# Optimizing a Trainium2 kernel written in Bass

```python
import numpy as np
import jax
import jax.numpy as jnp

def _softmax(x, axis=-1):
    return jax.nn.softmax(x, axis=axis)

def _gelu(x):
    return jax.nn.gelu(x, approximate=True)

def _silu(x):
    return jax.nn.silu(x)

def _sigmoid(x):
    return jax.nn.sigmoid(x)

def _layernorm(x, axis=-1, eps=1e-05):
    m = jnp.mean(x, axis=axis, keepdims=True)
    v = jnp.var(x, axis=axis, keepdims=True)
    return (x - m) / jnp.sqrt(v + eps)

def _scatter_add(tgt, idx, src, axis=0):
    return tgt.at[idx].add(src)

def _segment_sum(src, seg, n):
    return jax.ops.segment_sum(src, seg, n)
kernel_name = 'mk_pixart_resid_d1_seqx_r4_7c2d63'

def setup_inputs(seed: int=0):
    np.random.seed(seed)
    _w = jnp.asarray

    def _rec_inputs():
        import jax
        import jax.numpy as jnp
        _rk = jax.random.key(seed)
        x = -0.0002928 + 1 * jax.random.normal(jax.random.fold_in(_rk, 1), (2, 1024, 256), jnp.float32)
        _lenS = 1024 - jax.random.randint(jax.random.fold_in(_rk, 7), (2,), 0, max(1, 1024 // 4) + 1, jnp.int32)
        _lenS2 = 77 - jax.random.randint(jax.random.fold_in(_rk, 8), (2,), 0, max(1, 77 // 4) + 1, jnp.int32)
        _ctx_1024P = jax.random.normal(jax.random.fold_in(_rk, 11), (2, 16, 256), jnp.float32)
        _ctx_1024c = jax.random.dirichlet(jax.random.fold_in(_rk, 511), 0.3 * jnp.ones((16,), jnp.float32), (2, 77))
        _ctx_1024t = jnp.einsum('bsk,bkd->bsd', _ctx_1024c, _ctx_1024P)
        _ctx_1024t = _ctx_1024t * jax.lax.rsqrt(jnp.mean(jnp.square(_ctx_1024t)) + 1e-12) * 0.953939
        ctx_1024 = -1.39393e-06 + 0.999914 * (_ctx_1024t + 0.3 * jax.random.normal(jax.random.fold_in(_rk, 611), (2, 77, 256), jnp.float32))
        condB_tau = jax.random.uniform(jax.random.fold_in(_rk, 12), (2,), jnp.float32, 0.0, 1.23395)
        fside_BxS2_0 = -0.00205293 + 0.99739 * jax.random.normal(jax.random.fold_in(_rk, 13), (2, 77), jnp.float32)
        return (x, ctx_1024, condB_tau, fside_BxS2_0)
    x, ctx_1024, condB_tau, fside_BxS2_0 = _rec_inputs()

    def _L0_xcond_setup():
        import jax, jax.numpy as jnp
        import numpy as np
        B, S, D, H = (2, 512, 256, 16)
        DK = D // H

        def _split_heads(x):
            b, s, _ = x.shape
            return x.reshape(b, s, H, DK).transpose(0, 2, 1, 3)
        key = jax.random.key(seed)
        ks = jax.random.split(key, 14)
        inp = {'query': jax.random.normal(ks[0], (B, S, D), jnp.float32), 'key': jax.random.normal(ks[1], (B, S, D), jnp.float32), 'value': jax.random.normal(ks[2], (B, S, D), jnp.float32), 'tau': jax.random.uniform(ks[3], (B, 1), jnp.float32, 0.5, 1.5), 'delta': jax.random.normal(ks[4], (B, S), jnp.float32)}
        sc = 1.0 / np.sqrt(D)
        for i, name in enumerate(['q', 'k', 'v', 'o']):
            inp[f'W{name}'] = jax.random.normal(ks[5 + 2 * i], (D, D), jnp.float32) * sc
            inp[f'b{name}'] = jax.random.normal(ks[6 + 2 * i], (D,), jnp.float32) * 0.01
        return inp
    _L0_xcond_all = _L0_xcond_setup()
    _L0_xcond_in = {k: v for k, v in _L0_xcond_all.items() if k in ('Wq', 'bq', 'Wk', 'bk', 'Wv', 'bv', 'Wo', 'bo')}
    del _L0_xcond_all

    def _L0_ffn_setup():
        import jax, jax.numpy as jnp
        import numpy as np
        E = 8
        K = 2
        D = 256
        key = jax.random.key(seed)
        k0, k1, k2, k3 = jax.random.split(key, 4)
        x = jax.random.normal(k0, (2, 512, D), dtype=jnp.float32)
        gate_w = jax.random.normal(k1, (D, E), dtype=jnp.float32) * 0.02
        fc_w = jax.random.normal(k2, (E, D, 4 * D), dtype=jnp.float32) * 0.02
        proj_w = jax.random.normal(k3, (E, 4 * D, D), dtype=jnp.float32) * 0.02
        return {'x': x, 'gate_w': gate_w, 'fc_w': fc_w, 'proj_w': proj_w}
    _L0_ffn_all = _L0_ffn_setup()
    _L0_ffn_in = {k: v for k, v in _L0_ffn_all.items() if k in ('gate_w', 'fc_w', 'proj_w')}
    del _L0_ffn_all
    return {'x': x, 'ctx_1024': ctx_1024, 'condB_tau': condB_tau, 'fside_BxS2_0': fside_BxS2_0, 'L0_xcond_Wq': _L0_xcond_in['Wq'], 'L0_xcond_bq': _L0_xcond_in['bq'], 'L0_xcond_Wk': _L0_xcond_in['Wk'], 'L0_xcond_bk': _L0_xcond_in['bk'], 'L0_xcond_Wv': _L0_xcond_in['Wv'], 'L0_xcond_bv': _L0_xcond_in['bv'], 'L0_xcond_Wo': _L0_xcond_in['Wo'], 'L0_xcond_bo': _L0_xcond_in['bo'], 'L0_ffn_gate_w': _L0_ffn_in['gate_w'], 'L0_ffn_fc_w': _L0_ffn_in['fc_w'], 'L0_ffn_proj_w': _L0_ffn_in['proj_w']}

def reference(x, ctx_1024, condB_tau, fside_BxS2_0, L0_xcond_Wq, L0_xcond_bq, L0_xcond_Wk, L0_xcond_bk, L0_xcond_Wv, L0_xcond_bv, L0_xcond_Wo, L0_xcond_bo, L0_ffn_gate_w, L0_ffn_fc_w, L0_ffn_proj_w):
    import jax
    import jax.numpy as jnp

    def _L0_xcond_ref(query, key, value, tau, delta, Wq, bq, Wk, bk, Wv, bv, Wo, bo):
        import jax, jax.numpy as jnp
        import numpy as np
        B, S, D, H = (2, 512, 256, 16)
        DK = D // H

        def _split_heads(x):
            b, s, _ = x.shape
            return x.reshape(b, s, H, DK).transpose(0, 2, 1, 3)
        q = _split_heads(query @ Wq.T + bq)
        k = _split_heads(key @ Wk.T + bk)
        v = _split_heads(value @ Wv.T + bv)
        scores = jnp.einsum('bhqd,bhkd->bhqk', q, k)
        scores = scores * tau[:, :, None, None] + delta[:, None, None, :]
        scores = scores / jnp.sqrt(jnp.asarray(DK, scores.dtype))
        p_attn = jax.nn.softmax(scores, axis=-1)
        x = jnp.einsum('bhqk,bhkd->bhqd', p_attn, v)
        x = x.transpose(0, 2, 1, 3).reshape(query.shape[0], -1, H * DK)
        return x @ Wo.T + bo

    def _L0_ffn_ref(x, gate_w, fc_w, proj_w):
        import jax, jax.numpy as jnp
        import numpy as np
        E = 8
        K = 2
        D = 256
        orig_shape = x.shape
        d = orig_shape[-1]
        xt = x.reshape(-1, d)
        gates = jax.nn.softmax(xt @ gate_w, axis=-1)
        top_v, top_i = jax.lax.top_k(gates, K)
        top_v = top_v / jnp.sum(top_v, axis=-1, keepdims=True)
        h = jnp.einsum('nd,edf->enf', xt, fc_w)
        h = jax.nn.gelu(h, approximate=False)
        eo = jnp.einsum('enf,efd->end', h, proj_w)
        eo_nt = jnp.swapaxes(eo, 0, 1)
        sel = jnp.take_along_axis(eo_nt, top_i[:, :, None], axis=1)
        out = jnp.sum(sel * top_v[:, :, None], axis=1)
        return out.reshape(orig_shape)
    x = x + _L0_xcond_ref(_layernorm(x, axis=-1), ctx_1024, ctx_1024, condB_tau[:, None], fside_BxS2_0, L0_xcond_Wq, L0_xcond_bq, L0_xcond_Wk, L0_xcond_bk, L0_xcond_Wv, L0_xcond_bv, L0_xcond_Wo, L0_xcond_bo)
    x = x + _L0_ffn_ref(_layernorm(x, axis=-1), L0_ffn_gate_w, L0_ffn_fc_w, L0_ffn_proj_w)
    return x

_drawn_inputs = setup_inputs


def setup_inputs(seed=0):
    import zlib

    import numpy as np

    out = dict(_drawn_inputs(seed))
    spreads = {}
    factors = {'fside_BxS2_0': 2.922,
     'L0_xcond_bq': 51.714,
     'L0_xcond_bk': 64.0,
     'L0_xcond_bv': 5.152,
     'L0_xcond_bo': 6.132}
    for name, (base, spread) in spreads.items():
        noise = np.random.default_rng([zlib.crc32(name.encode()), seed]).standard_normal(out[name].shape)
        drawn = base * np.exp(spread * noise) if base else spread * noise
        out[name] = jnp.asarray(drawn.astype(out[name].dtype))
    for name, factor in factors.items():
        out[name] = (out[name] * factor).astype(out[name].dtype)
    return out
```

```python
from contextlib import ExitStack

import concourse.bass as bass
from concourse import mybir

F32 = mybir.dt.float32
F16 = mybir.dt.float16
BF16 = mybir.dt.bfloat16
I32 = mybir.dt.int32
U32 = mybir.dt.uint32
ALU = mybir.AluOpType
ACT = mybir.ActivationFunctionType
AX = mybir.AxisListType

P = 128
LN_EPS = 1e-5
W_SCALE = 64.0
H = 16
LIST_TILE = 256
LIST_PAD = LIST_TILE


class Chain:

    def __init__(self, eng, sem, base=0):
        self.eng, self.sem, self.base, self.n = eng, sem, base, 0

    def __call__(self, ins):
        self.n += 1
        ins.then_inc(self.sem, 1)
        self.eng.wait_ge(self.sem, self.base + self.n)


def settle(eng, passed):
    eng.sem_inc(passed, 1)


def build(nc, x, ctx_in, tau, fside, Wq, bq, Wk, bk, Wv, bv, Wo, bo, gate_w, fc_w, proj_w, out):
    B, S, D = x.shape
    KV = ctx_in.shape[1]
    E, _, F = fc_w.shape
    DK = D // H
    N = B * S
    T = 4
    BLK = T * P
    NBLK = N // BLK
    HALVES = S // BLK
    KD = D // P
    NG = H // 4
    U = NG * T
    CAP = N + LIST_PAD
    NT = (2 * N + E * (LIST_TILE - 1)) // LIST_TILE
    DUMMY = E * CAP
    ROW = D + 2
    SUB = LIST_TILE // P
    NP = F // (2 * P)
    WE = 2 * KD * F
    MAXT = N // LIST_TILE
    CH = 512
    assert (KD, DK, SUB, F // P, NBLK) == (2, 16, 2, 8, B * HALVES) and 2 * E * 4 * CH == NBLK * U * CH
    assert E * KD * F * 2 == NBLK * U * CH

    lists = nc.dram_tensor("lists", (E * CAP + LIST_TILE, ROW), F32, kind="Internal").ap()

    with ExitStack() as es:
        def sb(name, shape, dt=F32):
            return es.enter_context(nc.sbuf_tensor(name, shape, dt))

        def sem(name):
            return es.enter_context(nc.semaphore(name))

        ps = es.enter_context(nc.psum_tensor("ps", [P, 8, 512], F32))
        SCORE, PROBT, OUTB, SUMB, ODD = [0, 1, 2, 3], [4, 5], 6, 7, [2, 3]
        HID, YB, XB = [0, 1, 2, 3], [4, 5], [6, 7]

        ident = sb("ident", [P, P])
        tri = sb("tri", [P, P], BF16)
        ones_bf = sb("ones_bf", [P, P], BF16)
        head_mask = sb("head_mask", [P, 2, 4])
        iota_e = sb("iota_e", [P, E])
        pad_rows = sb("pad_rows", [P, SUB, ROW])
        fcw = sb("fcw", [P, E * WE], F16)
        prw = sb("prw", [P, E * WE], F16)
        gate = sb("gate", [P, KD, E])
        wqT = sb("wqT", [P, KD, D])
        woT = sb("woT", [P, KD, D])
        bq_sb = sb("bq_sb", [P, KD])
        bk_sb = sb("bk_sb", [P, KD])
        bo_sb = sb("bo_sb", [P, D])
        tau4 = sb("tau4", [P, B])
        w_stage = sb("w_stage", [P, 2, CH])
        kT = sb("kT", [P, KD, B, KV])
        v = sb("v", [KV, B, D])
        kbd = sb("kbd", [P, KD, 2, 4, KV])
        vpad = sb("vpad", [KV, H, 2 * DK])
        ones_pad = sb("ones_pad", [KV, 2, 2 * DK])
        dparts = sb("dparts", [3, B, KV], BF16)
        dcur = sb("dcur", [3, 4, KV], BF16)
        tau_cur = sb("tau_cur", [P, 1])
        x_in = sb("x_in", [P, T, D])
        x1 = sb("x1", [P, T, D])
        xnT = sb("xnT", [P, KD, BLK])
        qT = sb("qT", [P, KD, BLK])
        attnT = sb("attnT", [P, KD, BLK])
        probs = sb("probs", [P, 3, 4, KV])
        nmax = sb("nmax", [P, 2, 4])
        arena = sb("arena", [P, 4096])
        rows = sb("rows", [P, T, 2, ROW])
        stats = sb("stats", [P, T, 6])
        mv = sb("mv", [P, T, 2])
        ln = sb("ln", [P, 6, T])
        top8 = sb("top8", [P, T, 8])
        top8_at = sb("top8_at", [P, T, 8], U32)
        which = sb("which", [P, 2, T])
        chosen = sb("chosen", [P, 2, T, E])
        chosen_bf = sb("chosen_bf", [P, T, E], BF16)
        place_t = sb("place_t", [P, T, E])
        place = sb("place", [P, E])
        list_base = sb("list_base", [1, E])
        pos = sb("pos", [P, 2, T], I32)
        tw = sb("tw", [P, 4, T])
        row_no = sb("row_no", [P, T])
        tab_j = sb("tab_j", [1, E, MAXT])
        tab_jw = sb("tab_jw", [1, E, MAXT])
        tab_t = sb("tab_t", [1, NT, E])
        tab_w = sb("tab_w", [1, 3, NT, E])
        tab_s = sb("tab_s", [1, 6, E])
        tab_r = sb("tab_r", [1, 2, NT])
        tile_row = sb("tile_row", [1, NT], I32)
        tile_w = sb("tile_w", [1, NT], I32)
        pad_at = sb("pad_at", [1, E], I32)

        w_nat = arena[:, 0:2048].rearrange("p (w m d) -> p w m d", w=4, m=KD)
        wkvT = arena[:, 2048:3072].rearrange("p (w k d) -> p w k d", w=2, k=KD)
        ctx_nat = arena[0:KV, 3072:3584].rearrange("p (b d) -> p b d", b=B)
        ctxT = arena[:, 3584:3584 + KD * B * KV].rearrange("p (k n) -> p k n", k=KD)
        bv_sb = attnT[0:KV, 0, 0:D]
        d_row = attnT[0:1, 1, 0:B * KV]
        d_rest = qT[0:1, :, 0:B * KV]
        d_bf = qT[0:1, 0, 256:512].bitcast(BF16)
        d_bf3 = xnT[0:1, 0, 0:256].bitcast(BF16)[:, 0:3 * B * KV]
        probsT = arena[0:KV, :].rearrange("p (s j n) -> p s j n", s=2, j=4)
        h16 = arena[:, 0:2048].bitcast(F16).rearrange("p (s c n) -> p s c n", s=4, c=2)
        h32 = arena[:, 2048:3072].rearrange("p (s n) -> p s n", s=2)
        xT16 = arena[:, 3072:4096].bitcast(F16).rearrange("p (s c n) -> p s c n", s=2, c=2)
        x_list = rows[:, 0:2, :, :]
        y = x_in[:, :, :].rearrange("p (s h) d -> p s h d", s=2)
        y_row = sb("y_row", [P, 2, SUB], I32)
        y_scale = sb("y_scale", [P, 2, SUB])

        ctx_loaded, w_loaded, b_loaded, f_loaded = sem("ctx_loaded"), sem("w_loaded"), sem("b_loaded"), sem("f_loaded")
        x_loaded = sem("x_loaded")
        stage_loaded = [sem("stage_loaded0"), sem("stage_loaded1")]
        out_stored = sem("out_stored")
        consts_ready = sem("consts_ready")
        setup_pe, setup_act, setup_dve = sem("setup_pe"), sem("setup_act"), sem("setup_dve")
        d_split, d_moved = sem("d_split"), sem("d_moved")
        batch_ready, x_bias_added = sem("batch_ready"), sem("x_bias_added")
        pool_chain, dve_setup, dve_chain, act_chain, dve_tab = (
            sem("pool_chain"), sem("dve_setup"), sem("dve_chain"), sem("act_chain"), sem("dve_tab"))
        hid_high, pool_passed, dve_passed = sem("hid_high"), sem("pool_passed"), sem("dve_passed")
        var_ready, rstd_ready, xn_ready = sem("var_ready"), sem("rstd_ready"), sem("xn_ready")
        xT_made, xT_act, xT_dve, q_made, q_ready = sem("xT_made"), sem("xT_act"), sem("xT_dve"), sem("q_made"), sem("q_ready")
        scores_made, shifted, probs_ready = sem("scores_made"), sem("shifted"), sem("probs_ready")
        pT_made, pT_copied, pv_made, attn_ready = sem("pT_made"), sem("pT_copied"), sem("pv_made"), sem("attn_ready")
        o_made, x1_ready = sem("o_made"), sem("x1_ready")
        rows_ready, rows_copied, logits_made = sem("rows_ready"), sem("rows_copied"), sem("logits_made")
        gap_ready, exp_ready, chosen_ready, ranks_made = sem("gap_ready"), sem("exp_ready"), sem("chosen_ready"), sem("ranks_made")
        pos_ready, scattered, rows_free = sem("pos_ready"), sem("scattered"), sem("rows_free")
        w_high, w_rest = sem("w_high"), sem("w_rest")
        tables_ready, pads_written = sem("tables_ready"), sem("pads_written")
        list_loaded = [sem("list_loaded0"), sem("list_loaded1")]
        lx_made, lx_high, lx_rest = sem("lx_made"), sem("lx_high"), sem("lx_rest")
        hid_made, gelu_ready, hid_split, y_made, y_ready = (
            sem("hid_made"), sem("gelu_ready"), sem("hid_split"), sem("y_made"), sem("y_ready"))
        y_added, taken, adds_before = sem("y_added"), sem("taken"), sem("adds_before")

        def units():
            return [(m, par, t, (2 * m + par) * T + t) for m in range(KD) for par in range(2) for t in range(T)]

        def stage_dram(e, g, t):
            if g % 2 == 0:
                k, half = divmod(t, 2)
                return fc_w[bass.ds(e, 1), k * P:(k + 1) * P, half * CH:(half + 1) * CH].rearrange("e p n -> p (e n)")
            return proj_w[bass.ds(e, 1), 2 * t * P:(2 * t + 2) * P, :].rearrange("e (h p) n -> p (e h) n", p=P)

        def stage_sb(u, g):
            s = w_stage[:, u % 2, :]
            return s if g % 2 == 0 else s.rearrange("p (h n) -> p h n", h=2)

        def split_dst(e, g, t, part):
            if g % 2 == 0:
                k, half = divmod(t, 2)
                return fcw[:, bass.ds(e * WE + (2 * k + part) * F + half * CH, CH)]
            w = prw[:, :].rearrange("p (f c n) -> p f c n", c=2, n=D)
            return w[:, bass.ds(e * (F // P) + 2 * t, 2), part, :]

        block = es.enter_context(nc.Block())

        @block.sync
        def _(sp):
            for i, w in enumerate((Wk, Wv, Wq, Wo)):
                sp.dma_start(w_nat[:, i], w.rearrange("(m p) d -> p m d", p=P)).then_inc(w_loaded, 16)
            sp.dma_start(ctx_nat, ctx_in.rearrange("b k d -> k b d")).then_inc(ctx_loaded, 16)
            sp.dma_start(d_row, fside.rearrange("(a b) k -> a (b k)", a=1)).then_inc(f_loaded, 16)
            sp.dma_start(bk_sb[:], bk.rearrange("(m p) -> p m", p=P), allow_slow_non_contiguous=True).then_inc(b_loaded, 16)
            sp.dma_start(bq_sb[:], bq.rearrange("(m p) -> p m", p=P), allow_slow_non_contiguous=True).then_inc(b_loaded, 16)
            sp.dma_start(bv_sb, bv.rearrange("(a d) -> a d", a=1).to_broadcast([KV, D])).then_inc(b_loaded, 16)
            sp.dma_start(bo_sb[:], bo.rearrange("(a d) -> a d", a=1).to_broadcast([P, D])).then_inc(b_loaded, 16)
            sp.dma_start(tau4[:], tau.rearrange("(a b) -> a b", a=1).to_broadcast([P, B])).then_inc(b_loaded, 16)
            sp.dma_start(gate[:], gate_w.rearrange("(k p) e -> p k e", p=P)).then_inc(b_loaded, 16)
            sp.wait_ge(consts_ready, 1)
            sp.dma_start(out[N:N + LIST_PAD, :].rearrange("(h p) d -> p h d", p=P), pad_rows[:, :, 0:D]).then_inc(out_stored, 16)
            sp.dma_start(lists[DUMMY:DUMMY + LIST_TILE, :].rearrange("(h p) r -> p h r", p=P), pad_rows[:]).then_inc(pads_written, 16)
            x_rows = x.rearrange("b s d -> (b s) d")
            with sp.Fori(0, NBLK) as k:
                sp.wait_ge(x1_ready, k + 1)
                sp.dma_start(x_in[:], x_rows[bass.ds(k * BLK, BLK), :].rearrange("(t p) d -> p t d", p=P)).then_inc(x_loaded, 16)
                for m, par, t, u in units():
                    g = 2 * m + par
                    sp.wait_ge(w_rest, U * k + u + 1)
                    sp.dma_start(stage_sb(u, g), stage_dram(2 * k + g // 2, g, t)).then_inc(stage_loaded[u % 2], 16)
                sp.wait_ge(x1_ready, k + 2)
                sp.dma_start(out[bass.ds(k * BLK, BLK), :].rearrange("(t p) d -> p t d", p=P), x1[:]).then_inc(out_stored, 16)
            sp.wait_ge(tables_ready, 1)
            for e in range(E):
                at = sp.value_load(pad_at[0:1, e:e + 1], min_val=e * CAP, max_val=e * CAP + N)
                sp.dma_start(lists[bass.ds(at, LIST_PAD), :].rearrange("(h p) r -> p h r", p=P), pad_rows[:]).then_inc(pads_written, 16)
            sp.wait_ge(pads_written, 16 * (E + 1))
            sp.wait_ge(scattered, 16 * 2 * T * NBLK)

            def load_tile(t, slot):
                at = sp.value_load(tile_row[0:1, bass.ds(t, 1)], min_val=0, max_val=DUMMY)
                sp.dma_start(x_list[:, slot], lists[bass.ds(at, LIST_TILE), :].rearrange("(h p) r -> p h r", p=P)).then_inc(list_loaded[slot], 16)

            load_tile(0, 0)
            load_tile(1, 1)
            with sp.Fori(0, (NT - 2) // 2) as i:
                for s in range(2):
                    sp.wait_ge(lx_made, 2 * i + s + 1)
                    sp.wait_ge(taken, 2 * i + s + 1)
                    load_tile(2 * i + s + 2, s)
            for t in range(2 + (NT - 2) // 2 * 2, NT):
                sp.wait_ge(lx_made, t - 1)
                sp.wait_ge(taken, t - 1)
                load_tile(t, t % 2)
            sp.wait_ge(out_stored, 16 * (NBLK + 1))
            sp.wait_ge(y_added, 16 * SUB * NT)

        @block.gpsimd
        def _(pool):
            link = Chain(pool, pool_chain)
            link(pool.memset(pad_rows[:], 0.0))
            link(pool.iota(pad_rows[:, :, D + 1:D + 2].bitcast(I32), pattern=[[P, SUB], [0, 1]], base=N, channel_multiplier=1))
            link(pool.memset(ident[:], 0.0))
            link(pool.affine_select(out=ident[:], in_=ident[:], compare_op=ALU.not_equal, fill=1.0, base=0,
                                    pattern=[[-1, P]], channel_multiplier=1))
            pool.sem_inc(consts_ready, 1)
            link(pool.memset(ones_bf[:], 1.0))
            link(pool.memset(tri[:], 1.0))
            link(pool.affine_select(out=tri[:], in_=tri[:], compare_op=ALU.is_gt, fill=0.0, base=0,
                                    pattern=[[1, P]], channel_multiplier=-1))
            link(pool.memset(head_mask[:], 1.0))
            link(pool.affine_select(out=head_mask[:], in_=head_mask[:], compare_op=ALU.is_ge, fill=0.0, base=0,
                                    pattern=[[-DK, 2], [-2 * DK, 4]], channel_multiplier=1))
            link(pool.affine_select(out=head_mask[:], in_=head_mask[:], compare_op=ALU.is_ge, fill=0.0, base=DK - 1,
                                    pattern=[[DK, 2], [2 * DK, 4]], channel_multiplier=-1))
            for dst, base_step in ((iota_e, 1), (place, CAP), (list_base, CAP)):
                link(pool.iota(dst[:], pattern=[[base_step, E]], base=0, channel_multiplier=0, allow_small_or_imprecise_dtypes=True))
            link(pool.iota(row_no[:], pattern=[[P, T]], base=0, channel_multiplier=1, allow_small_or_imprecise_dtypes=True))
            link(pool.iota(tab_j[:], pattern=[[0, E], [LIST_TILE, MAXT]], base=0, channel_multiplier=0, allow_small_or_imprecise_dtypes=True))
            link(pool.iota(tab_t[:], pattern=[[1, NT], [0, E]], base=0, channel_multiplier=0, allow_small_or_imprecise_dtypes=True))
            link(pool.memset(ones_pad[:], 0.0))
            link(pool.memset(vpad[:], 0.0))
            for par in range(2):
                link(pool.memset(ones_pad[:, par, par * DK:(par + 1) * DK], 1.0))
            pool.sem_inc(consts_ready, 1)
            pool.sem_inc(rows_free, 1)

            with pool.Fori(0, B) as b:
                pool.wait_ge(attn_ready, 2 * KD * b + 2 * KD)
                pool.wait_ge(setup_act, 7)
                pool.wait_ge(setup_dve, 2)
                for m in range(KD):
                    pool.tensor_tensor(kbd[:, m].rearrange("p a j k -> p (a j) k"),
                                       kT[:, m, bass.ds(b, 1), :].to_broadcast([P, 8, KV]),
                                       head_mask[:].rearrange("p a (j o) -> p (a j) o", o=1).to_broadcast([P, 8, KV]), ALU.mult)
                for par in range(2):
                    pool.tensor_copy(vpad[:, par::2, par * DK:(par + 1) * DK],
                                     v[:, bass.ds(b, 1), :].rearrange("p b (h d) -> p (b h) d", h=H)[:, par::2, :])
                pool.wait_ge(d_moved, 48)
                pool.tensor_copy(dcur[:], dparts[:, bass.ds(b, 1), :].to_broadcast([3, 4, KV])).then_inc(batch_ready, 1)
                with pool.Fori(0, HALVES) as half:
                    k = b * HALVES + half
                    pool.wait_ge(xn_ready, k + 1)
                    pool.tensor_tensor(x_in[:], x_in[:], bo_sb[:].rearrange("p (o d) -> p o d", o=1).to_broadcast([P, T, D]), ALU.add).then_inc(x_bias_added, 1)
                    pool.wait_ge(rows_ready, k + 1)
                    settle(pool, pool_passed)
                    pool.tensor_copy(rows[:, :, 1, 0:D], rows[:, :, 0, 0:D]).then_inc(rows_copied, 1)
                    pool.wait_ge(rows_copied, k + 1)
                    pool.wait_ge(pos_ready, k + 1)
                    settle(pool, pool_passed)
                    for s in range(2):
                        for t in range(T):
                            pool.indirect_dma_start(lists[:, :], bass.IndirectOffsetOnAxis(ap=pos[:, s, t:t + 1], axis=0),
                                                    rows[:, t, s, :], None).then_inc(scattered, 16)
                    pool.wait_ge(scattered, 16 * 2 * T * (k + 1))
                    pool.sem_inc(rows_free, 1)
            pool.wait_ge(out_stored, 16 * (NBLK + 1))

            def add_tile(t, s, first=False):
                if not first:
                    pool.wait_ge(y_added, 16 * SUB * t)
                pool.sem_inc(adds_before, 1)
                pool.wait_ge(y_ready, t + 1)
                settle(pool, pool_passed)
                for h in range(SUB):
                    pool.indirect_dma_start(out[:, :], bass.IndirectOffsetOnAxis(ap=y_row[:, s, h:h + 1], axis=0),
                                            y[:, s, h, :], None, compute_op=ALU.add).then_inc(y_added, 16)

            add_tile(0, 0, first=True)
            with pool.Fori(0, (NT - 1) // 2) as i:
                for s2 in range(2):
                    add_tile(2 * i + s2 + 1, (s2 + 1) % 2)
            pool.wait_ge(y_added, 16 * SUB * NT)

        @block.tensor
        def _(pe):
            pe.wait_ge(consts_ready, 1)
            pe.wait_ge(w_loaded, 64)
            for w in range(4):
                for k in range(KD):
                    for m in range(KD):
                        last = pe.transpose(ps[:, w, k * D + m * P:k * D + (m + 1) * P], w_nat[:, w, m, k * P:(k + 1) * P], ident[:])
                last.then_inc(setup_pe, 1)
            pe.wait_ge(ctx_loaded, 16)
            for k in range(KD):
                for b in range(B):
                    last = pe.transpose(ps[:, 4, (k * B + b) * KV:(k * B + b + 1) * KV], ctx_nat[:, b, k * P:(k + 1) * P], ident[0:KV, 0:KV])
            last.then_inc(setup_pe, 1)
            pe.wait_ge(setup_act, 5)
            for m in range(KD):
                for k in range(KD):
                    last = pe.matmul(ps[:, 5 + m, 0:B * KV], wkvT[:, 0, k, m * P:(m + 1) * P], ctxT[:, k, :], start=(k == 0), stop=(k == KD - 1))
                last.then_inc(setup_pe, 1)
            for b in range(B):
                for k in range(KD):
                    last = pe.matmul(ps[0:KV, 7 if b else 4, 0:D], ctxT[:, k, b * KV:(b + 1) * KV], wkvT[:, 1, k, :], start=(k == 0), stop=(k == KD - 1))
                last.then_inc(setup_pe, 1)
            pe.wait_ge(setup_act, 7)
            pe.wait_ge(setup_dve, 2)
            pe.wait_ge(consts_ready, 2)

            with pe.Fori(0, NBLK) as blk:
                def transposed(src, n):
                    for k in range(KD):
                        for t in range(T):
                            last = pe.transpose(ps[:, ODD[k], t * P:(t + 1) * P], rows[:, t, 0, k * P:(k + 1) * P], ident[:])
                        last.then_inc(xT_made, 1)
                    pe.wait_ge(xT_act, 2 * blk + n)
                    pe.wait_ge(xT_dve, 2 * blk + n)

                pe.wait_ge(xn_ready, blk + 1)
                transposed(rows, 1)
                for m in range(KD):
                    for k in range(KD):
                        last = pe.matmul(ps[:, ODD[m], :], wqT[:, k, m * P:(m + 1) * P], xnT[:, k, :], start=(k == 0), stop=(k == KD - 1))
                    last.then_inc(q_made, 1)
                pe.wait_ge(batch_ready, (blk + HALVES) // HALVES)

                def scores(u):
                    m, par, t, _ = units()[u]
                    if u == 0:
                        pe.wait_ge(q_ready, KD * blk + 1)
                    if u == 2:
                        pe.wait_ge(q_ready, KD * blk + KD)
                    if u >= len(SCORE):
                        pe.wait_ge(shifted, U * blk + u - len(SCORE) + 1)
                    o = ps[:, SCORE[u % len(SCORE)], 0:4 * KV]
                    pe.matmul(o, ones_bf[0:3, :], dcur[:].rearrange("p j k -> p (j k)"), start=True, stop=False)
                    pe.matmul(o, qT[:, m, t * P:(t + 1) * P], kbd[:, m, par].rearrange("p j k -> p (j k)"), start=False, stop=True).then_inc(scores_made, 1)

                def transpose_probs(u):
                    pe.wait_ge(probs_ready, U * blk + u + 1)
                    if u >= 2:
                        pe.wait_ge(pT_copied, U * blk + u - 1)
                    for j in range(4):
                        last = pe.transpose(ps[0:KV, PROBT[u % 2], j * P:(j + 1) * P], probs[:, u % 3, j, :], ident[:])
                    last.then_inc(pT_made, 1)

                def weigh_values(g):
                    m, par = divmod(g, 2)
                    pe.wait_ge(pT_copied, U * blk + T * (g + 1))
                    if g == 2:
                        pe.wait_ge(attn_ready, KD * blk + 1 + 2 * KD)
                    for bank, w in ((OUTB, None), (SUMB, ones_pad[:, par, :])):
                        for j in range(4):
                            wt = vpad[:, 8 * m + 2 * j + par, :] if w is None else w
                            last = pe.matmul(ps[2 * DK * j:2 * DK * (j + 1), bank, :], wt, probsT[:, g % 2, j, :], start=(par == 0), stop=(par == 1))
                    last.then_inc(pv_made, 1)

                scores(0)
                scores(1)
                for u in range(U):
                    if u + 2 < U:
                        scores(u + 2)
                    transpose_probs(u)
                    if u % T == 0 and u:
                        weigh_values(u // T - 1)
                weigh_values(NG - 1)
                pe.wait_ge(attn_ready, KD * blk + KD + 2 * KD)
                for t in range(T):
                    for m in range(KD):
                        last = pe.matmul(ps[:, ODD[t // 2], (t % 2) * D:(t % 2 + 1) * D], attnT[:, m, t * P:(t + 1) * P], woT[:, m, :],
                                         start=(m == 0), stop=(m == KD - 1))
                    if t % 2:
                        last.then_inc(o_made, 1)
                pe.wait_ge(rows_ready, blk + 1)
                transposed(rows, 2)
                for t in range(T):
                    for k in range(KD):
                        last = pe.matmul(ps[:, ODD[0], t * E:(t + 1) * E], xnT[:, k, t * P:(t + 1) * P], gate[:, k, :], start=(k == 0), stop=(k == KD - 1))
                last.then_inc(logits_made, 1)
                pe.wait_ge(chosen_ready, blk + 1)
                c = chosen_bf[:].rearrange("p t e -> p (t e)")
                pe.matmul(ps[:, ODD[0], 0:T * E], tri[:], c, start=True, stop=False, skip_group_check=True)
                for t in range(T - 1):
                    later = T - 1 - t
                    pe.matmul(ps[:, ODD[0], (t + 1) * E:T * E].rearrange("p (t e) -> p t e", e=E), ones_bf[:],
                              chosen_bf[:, t:t + 1, :].to_broadcast([P, later, E]), start=False, stop=(t == T - 2), skip_group_check=True)
                for t in range(T):
                    last = pe.matmul(ps[:, ODD[1], 0:E], ones_bf[:], chosen_bf[:, t, :], start=(t == 0), stop=(t == T - 1))
                last.then_inc(ranks_made, 1)

            pe.wait_ge(tables_ready, 1)
            pe.wait_ge(w_high, NBLK * U)
            pe.wait_ge(w_rest, NBLK * U + 2)

            def list_rows(t, s, n):
                pe.wait_ge(list_loaded[s], 16 * n)
                for k in range(KD):
                    for h in range(SUB):
                        last = pe.transpose(ps[:, XB[s], (k * SUB + h) * P:(k * SUB + h + 1) * P], x_list[:, s, h, k * P:(k + 1) * P], ident[:])
                last.then_inc(lx_made, 1)

            def hidden(t, s, step, w):
                if step == 0:
                    pe.wait_ge(lx_rest, t + 1)
                for f2 in range(2):
                    f = 2 * step + f2
                    o = ps[:, HID[step], f2 * LIST_TILE:(f2 + 1) * LIST_TILE]
                    n = 0
                    for k in range(KD):
                        for wp, xp in ((0, 0), (0, 1), (1, 0)):
                            last = pe.matmul(o, fcw[:, bass.ds(w + ((2 * k + wp) * F + f * P), P)],
                                             xT16[:, s, xp, k * LIST_TILE:(k + 1) * LIST_TILE], start=(n == 0), stop=(n == 3 * KD - 1))
                            n += 1
                last.then_inc(hid_made, 1)

            def outputs(t, s, step, w):
                pe.wait_ge(hid_split, NP * t + step + 1)
                for f2 in range(2):
                    for wp, hp in ((0, 0), (0, 1), (1, 0)):
                        for h in range(SUB):
                            first = (step, f2, wp, hp, h) == (0, 0, 0, 0, 0)
                            final = (step, f2, wp) == (NP - 1, 1, 1)
                            last = pe.matmul(ps[:, YB[s], h * D:(h + 1) * D],
                                             h16[:, step, hp, f2 * LIST_TILE + h * P:f2 * LIST_TILE + (h + 1) * P],
                                             prw[:, bass.ds(w + (2 * (2 * step + f2) + wp) * D, D)],
                                             start=first, stop=final, skip_group_check=True)
                if step == NP - 1:
                    last.then_inc(y_made, 1)

            def weights_of(t):
                return pe.value_load(tile_w[0:1, bass.ds(t, 1)], min_val=0, max_val=(E - 1) * WE)

            LAG = 2

            def tile(t, s, w_last, more=True):
                w = weights_of(t)
                for step in range(NP):
                    hidden(t, s, step, w)
                    if step == 1 and more:
                        list_rows(t + 1, 1 - s, (t + 3) // 2)
                    if step >= LAG:
                        outputs(t, s, step - LAG, w)
                    elif w_last is not None:
                        outputs(t - 1, 1 - s, NP - LAG + step, w_last)

            list_rows(0, 0, 1)
            tile(0, 0, None)
            with pe.Fori(0, (NT - 3) // 2) as i:
                for s2 in range(2):
                    tile(2 * i + (s2 + 1), 1 - s2, weights_of(2 * i + s2))
            for t in range(NT - 2, NT):
                tile(t, t % 2, weights_of(t - 1), more=t < NT - 1)
            w = weights_of(NT - 1)
            for step in range(NP - LAG, NP):
                outputs(NT - 1, (NT - 1) % 2, step, w)

        @block.scalar
        def _(act):
            for i, dst in enumerate((wkvT[:, 0], wkvT[:, 1], wqT[:], woT[:])):
                act.wait_ge(setup_pe, i + 1)
                act.copy(dst, ps[:, i, :].rearrange("p (k d) -> p k d", k=KD)).then_inc(setup_act, 1)
            act.wait_ge(setup_pe, 5)
            act.copy(ctxT, ps[:, 4, 0:KD * B * KV].rearrange("p (k n) -> p k n", k=KD)).then_inc(setup_act, 1)
            act.wait_ge(b_loaded, 96)
            for m in range(KD):
                act.wait_ge(setup_pe, 6 + m)
                act.activation(kT[:, m].rearrange("p b k -> p (b k)"), ps[:, 5 + m, 0:B * KV], ACT.Identity, bias=bk_sb[:, m:m + 1]).then_inc(setup_act, 1)
            for i in range(3):
                act.wait_ge(d_split, 1)
                act.dma_start(dparts[i:i + 1, :, :].rearrange("p b k -> p (b k)"), d_bf3[:, i * B * KV:(i + 1) * B * KV]).then_inc(d_moved, 16)

            with act.Fori(0, NBLK) as blk:
                link = Chain(act, act_chain, 2 * blk)

                def rsqrt_start(n):
                    act.wait_ge(var_ready, 2 * blk + n)
                    link(act.activation(ln[:, 1, :], ln[:, 0, :], ACT.Ln))
                    act.activation(ln[:, 2, :], ln[:, 1, :], ACT.Exp, scale=-0.5).then_inc(rstd_ready, 1)

                def copy_rows(n):
                    act.wait_ge(xT_made, 4 * blk + 2 * n - 1)
                    act.copy(xnT[:, 0, :], ps[:, ODD[0], :]).then_inc(xT_act, 1)

                rsqrt_start(1)
                copy_rows(1)

                def copy_probs(u):
                    act.wait_ge(pT_made, U * blk + u + 1)
                    g, t = divmod(u, T)
                    if g >= 2 and t == 0:
                        act.wait_ge(pv_made, NG * blk + g - 1)
                    act.copy(probsT[:, g % 2, :, t * P:(t + 1) * P], ps[0:KV, PROBT[u % 2], :].rearrange("p (j n) -> p j n", j=4)).then_inc(pT_copied, 1)

                for m, par, t, u in units():
                    g = 2 * m + par
                    act.wait_ge(shifted, U * blk + u + 1)
                    act.activation(probs[:, u % 3], probs[:, u % 3], ACT.Exp).then_inc(probs_ready, 1)
                    act.wait_ge(stage_loaded[u % 2], 16 * (U // 2 * blk + u // 2 + 1))
                    act.activation(split_dst(2 * blk + g // 2, g, t, 0), stage_sb(u, g), ACT.Copy, scale=W_SCALE).then_inc(w_high, 1)
                    if u >= 1:
                        copy_probs(u - 1)
                copy_probs(U - 1)
                rsqrt_start(2)
                copy_rows(2)
                act.wait_ge(gap_ready, blk + 1)
                act.activation(tw[:, 1, :], tw[:, 0, :], ACT.Exp).then_inc(exp_ready, 1)

            def row_high(t, s):
                act.wait_ge(lx_made, t + 1)
                act.copy(xT16[:, s, 0, :], ps[:, XB[s], :]).then_inc(lx_high, 1)

            def gelu(t, step, first=False):
                act.wait_ge(hid_made, NP * t + step + 1)
                if not (first and step < 2):
                    act.wait_ge(hid_split, NP * t + step - 1)
                act.activation(h32[:, step % 2, :], ps[:, HID[step], :], ACT.Gelu, scale=1.0 / W_SCALE).then_inc(gelu_ready, 1)

            def tile(t, s, first=False, more=True):
                for step in range(NP):
                    gelu(t, step, first)
                    if step == 1 and more:
                        row_high(t + 1, 1 - s)

            row_high(0, 0)
            tile(0, 0, first=True)
            with act.Fori(0, (NT - 3) // 2) as i:
                for s2 in range(2):
                    tile(2 * i + (s2 + 1), 1 - s2)
            for t in range(NT - 2, NT):
                tile(t, t % 2, more=t < NT - 1)

        @block.vector
        def _(dve):
            link = Chain(dve, dve_setup)
            dve.sem_inc(w_rest, 2)
            dve.sem_inc(x1_ready, 1)
            dve.sem_inc(attn_ready, 2 * KD)
            dve.wait_ge(f_loaded, 16)
            link(dve.tensor_scalar(d_rest[:, 0], d_row, 0.25, None, ALU.mult))
            link(dve.tensor_copy(d_bf3[:, 0:B * KV], d_rest[:, 0]))
            link(dve.tensor_tensor(d_rest[:, 1], d_rest[:, 0], d_bf3[:, 0:B * KV], ALU.subtract))
            link(dve.tensor_copy(d_bf3[:, B * KV:2 * B * KV], d_rest[:, 1]))
            link(dve.tensor_tensor(d_rest[:, 0], d_rest[:, 1], d_bf3[:, B * KV:2 * B * KV], ALU.subtract))
            dve.tensor_copy(d_bf3[:, 2 * B * KV:3 * B * KV], d_rest[:, 0]).then_inc(d_split, 1)
            dve.wait_ge(b_loaded, 96)
            for b in range(B):
                dve.wait_ge(setup_pe, 8 + b)
                dve.tensor_tensor(v[:, b, :], ps[0:KV, 7 if b else 4, 0:D], bv_sb, ALU.add).then_inc(setup_dve, 1)
            dve.wait_ge(d_moved, 48)
            dve.wait_ge(consts_ready, 2)
            DVE_CHAIN = 42

            with dve.Fori(0, NBLK) as blk:
                link = Chain(dve, dve_chain, DVE_CHAIN * blk)

                def normalise(src, n):
                    for t in range(T):
                        last = dve.bn_stats(stats[:, t, :], src[:, t, :])
                    link(last)
                    settle(dve, dve_passed)
                    for t in range(T):
                        last = dve.bn_aggr(mv[:, t, :], stats[:, t, :])
                    link(last)
                    dve.tensor_scalar(ln[:, 0, :], mv[:, :, 1], LN_EPS, None, ALU.add).then_inc(var_ready, 1)
                    dve.wait_ge(rstd_ready, 2 * blk + n)
                    link(dve.tensor_tensor(ln[:, 3, :], ln[:, 2, :], ln[:, 2, :], ALU.mult))
                    link(dve.tensor_tensor(ln[:, 4, :], ln[:, 3, :], ln[:, 0, :], ALU.mult))
                    link(dve.tensor_scalar(ln[:, 3, :], ln[:, 4, :], -0.5, 1.5, ALU.mult, ALU.add))
                    link(dve.tensor_tensor(ln[:, 5, :], ln[:, 3, :], ln[:, 2, :], ALU.mult))
                    for t in range(T):
                        last = dve.tensor_scalar(rows[:, t, 0, 0:D], src[:, t, :], mv[:, t, 0:1], ln[:, 5, t:t + 1], ALU.subtract, ALU.mult)
                    return last

                def copy_rows(n):
                    dve.wait_ge(xT_made, 4 * blk + 2 * n)
                    dve.tensor_copy(xnT[:, 1, :], ps[:, ODD[1], :]).then_inc(xT_dve, 1)

                dve.wait_ge(x_loaded, 16 * (blk + 1))
                dve.wait_ge(rows_free, blk + 1)
                normalise(x_in, 1).then_inc(xn_ready, 1)
                copy_rows(1)
                link(dve.tensor_scalar(tau_cur[:], tau4[:, bass.ds(blk // HALVES, 1)], 0.25, None, ALU.mult))
                for m in range(KD):
                    dve.wait_ge(q_made, KD * blk + m + 1)
                    dve.tensor_scalar(qT[:, m, :], ps[:, ODD[m], :], bq_sb[:, m:m + 1], tau_cur[:, 0:1], ALU.add, ALU.mult).then_inc(q_ready, 1)

                def weight_rest(u):
                    g, t = divmod(u, T)
                    dve.wait_ge(w_high, U * blk + u + 1)
                    dve.scalar_tensor_tensor(out=split_dst(2 * blk + g // 2, g, t, 1), in0=stage_sb(u, g), scalar=W_SCALE,
                                             in1=split_dst(2 * blk + g // 2, g, t, 0), op0=ALU.mult, op1=ALU.subtract).then_inc(w_rest, 1)

                def divide(m):
                    dve.wait_ge(pv_made, NG * blk + 2 * m + 2)
                    link(dve.reciprocal(attnT[:, m, :], ps[:, SUMB, :]))
                    dve.tensor_tensor(attnT[:, m, :], ps[:, OUTB, :], attnT[:, m, :], ALU.mult).then_inc(attn_ready, 1)

                for m, par, t, u in units():
                    s = ps[:, SCORE[u % len(SCORE)], 0:4 * KV].rearrange("p (j k) -> p j k", j=4)
                    dve.wait_ge(scores_made, U * blk + u + 1)
                    link(dve.tensor_reduce(nmax[:, u % 2, :], s, AX.X, ALU.max, negate=True))
                    if u >= 3:
                        dve.wait_ge(pT_made, U * blk + u - 2)
                    dve.tensor_tensor(probs[:, u % 3], s, nmax[:, u % 2, :].rearrange("p (j o) -> p j o", o=1).to_broadcast([P, 4, KV]), ALU.add).then_inc(shifted, 1)
                    if u >= 1:
                        weight_rest(u - 1)
                    if u == 2 * T + 2:
                        divide(0)
                weight_rest(U - 1)
                divide(1)

                dve.wait_ge(x_bias_added, blk + 1)
                dve.wait_ge(out_stored, 16 * (blk + 1))
                for i in range(2):
                    dve.wait_ge(o_made, 2 * blk + i + 1)
                    last = dve.tensor_tensor(x1[:, 2 * i:2 * i + 2, :], ps[:, ODD[i], :].rearrange("p (t d) -> p t d", t=2), x_in[:, 2 * i:2 * i + 2, :], ALU.add)
                last.then_inc(x1_ready, 1)
                dve.wait_ge(x1_ready, blk + 2)
                normalise(x1, 2).then_inc(rows_ready, 1)
                copy_rows(2)
                dve.wait_ge(logits_made, blk + 1)
                settle(dve, dve_passed)
                lg = ps[:, ODD[0], 0:T * E].rearrange("p (t e) -> p t e", t=T)
                for t in range(T):
                    last = dve.max(top8[:, t, :], lg[:, t, :])
                link(last)
                settle(dve, dve_passed)
                for t in range(T):
                    last = dve.max_index(top8_at[:, t, :], top8[:, t, :], lg[:, t, :])
                link(last)
                dve.tensor_tensor(tw[:, 0, :], top8[:, :, 1], top8[:, :, 0], ALU.subtract).then_inc(gap_ready, 1)
                link(dve.tensor_copy(which[:].rearrange("p s t -> p t s"), top8_at[:, :, 0:2]))
                for s in range(2):
                    last = dve.tensor_tensor(chosen[:, s], which[:, s, :].rearrange("p (t o) -> p t o", o=1).to_broadcast([P, T, E]),
                                             iota_e[:].rearrange("p (o e) -> p o e", o=1).to_broadcast([P, T, E]), ALU.is_equal)
                link(last)
                dve.tensor_tensor(chosen_bf[:], chosen[:, 0], chosen[:, 1], ALU.add).then_inc(chosen_ready, 1)
                dve.wait_ge(exp_ready, blk + 1)
                link(dve.tensor_scalar(tw[:, 2, :], tw[:, 1, :], 1.0, None, ALU.add))
                link(dve.reciprocal(tw[:, 3, :], tw[:, 2, :]))
                dve.tensor_copy(rows[:, :, 0, D], tw[:, 3, :])
                dve.tensor_tensor(rows[:, :, 1, D], tw[:, 1, :], tw[:, 3, :], ALU.mult)
                for s in range(2):
                    last = dve.tensor_copy(rows[:, :, s, D + 1].bitcast(I32), row_no[:])
                link(last)
                dve.tensor_scalar(row_no[:], row_no[:], float(BLK), None, ALU.add)
                dve.wait_ge(ranks_made, blk + 1)
                link(dve.tensor_tensor(place_t[:], ps[:, ODD[0], 0:T * E].rearrange("p (t e) -> p t e", t=T),
                                       place[:].rearrange("p (o e) -> p o e", o=1).to_broadcast([P, T, E]), ALU.add))
                for s in range(2):
                    last = dve.tensor_tensor(chosen[:, s], chosen[:, s], place_t[:], ALU.mult)
                link(last)
                for s in range(2):
                    last = dve.tensor_reduce(which[:, s, :], chosen[:, s], AX.X, ALU.add)
                link(last)
                dve.tensor_copy(pos[:], which[:]).then_inc(pos_ready, 1)
                link(dve.tensor_tensor(place[:], ps[:, ODD[1], 0:E], place[:], ALU.add))
                chain_steps = link.n
            assert chain_steps == DVE_CHAIN, chain_steps

            link = Chain(dve, dve_tab)
            length, tiles, end, begin, shift, one = (tab_s[:, i, :] for i in range(6))
            dve.memset(one, 1.0)
            dve.tensor_copy(pad_at[:], place[0:1, :])
            link(dve.tensor_tensor(length, place[0:1, :], list_base[:], ALU.subtract))
            link(dve.tensor_tensor(tab_jw[:], length.rearrange("p (e o) -> p e o", o=1).to_broadcast([1, E, MAXT]), tab_j[:], ALU.is_gt))
            link(dve.tensor_reduce(tiles, tab_jw[:], AX.X, ALU.add))
            link(dve.tensor_tensor_scan(end, one, tiles, 0.0, ALU.mult, ALU.add))
            link(dve.tensor_tensor(begin, end, tiles, ALU.subtract))
            link(dve.tensor_scalar(shift, begin, -float(LIST_TILE), -float(DUMMY), ALU.mult, ALU.add))
            link(dve.tensor_tensor(shift, shift, list_base[:], ALU.add))

            def over_tiles(row):
                return row.rearrange("p (o e) -> p o e", o=1).to_broadcast([1, NT, E])

            dve.tensor_tensor(tab_w[:, 0], over_tiles(begin), tab_t[:], ALU.is_le)
            link(dve.tensor_tensor(tab_w[:, 1], over_tiles(end), tab_t[:], ALU.is_le))
            dve.tensor_reduce(tab_r[:, 0, :], tab_w[:, 1], AX.X, ALU.add)
            dve.tensor_tensor(tab_w[:, 0], tab_w[:, 0], tab_w[:, 1], ALU.subtract)
            link(dve.scalar_tensor_tensor(out=tab_w[:, 2], in0=tab_t[:], scalar=float(LIST_TILE), in1=over_tiles(shift), op0=ALU.mult, op1=ALU.add))
            link(dve.tensor_tensor(tab_w[:, 2], tab_w[:, 2], tab_w[:, 0], ALU.mult))
            link(dve.tensor_reduce(tab_r[:, 1, :], tab_w[:, 2], AX.X, ALU.add))
            dve.tensor_scalar(tile_row[:], tab_r[:, 1, :], float(DUMMY), None, ALU.add)
            link(dve.tensor_scalar(tile_w[:], tab_r[:, 0, :], float(E - 1), float(WE), ALU.min, ALU.mult))
            dve.sem_inc(tables_ready, 1)

            def row_rest(t, s):
                dve.wait_ge(lx_high, t + 1)
                dve.tensor_tensor(xT16[:, s, 1, :], ps[:, XB[s], :], xT16[:, s, 0, :], ALU.subtract).then_inc(lx_rest, 1)

            def take_weights(t, s, n, first=False):
                dve.wait_ge(list_loaded[s], 16 * n)
                if not first:
                    dve.wait_ge(adds_before, t)
                dve.tensor_copy(y_row[:, s, :], x_list[:, s, :, D + 1].bitcast(I32))
                dve.tensor_scalar(y_scale[:, s, :], x_list[:, s, :, D], 1.0 / W_SCALE, None, ALU.mult).then_inc(taken, 1)

            def split_hidden(t, step):
                dve.wait_ge(gelu_ready, NP * t + step + 1)
                dve.tensor_copy(h16[:, step, 0, :], h32[:, step % 2, :]).then_inc(hid_high, 1)
                dve.wait_ge(hid_high, NP * t + step + 1)
                dve.tensor_tensor(h16[:, step, 1, :], h32[:, step % 2, :], h16[:, step, 0, :], ALU.subtract).then_inc(hid_split, 1)

            def results(t, s):
                dve.wait_ge(y_made, t + 1)
                for h in range(SUB):
                    last = dve.tensor_scalar(y[:, s, h, :], ps[:, YB[s], h * D:(h + 1) * D], y_scale[:, s, h:h + 1], None, ALU.mult)
                last.then_inc(y_ready, 1)

            def tile(t, s, first=False, more=True):
                for step in range(NP):
                    split_hidden(t, step)
                    if step == 1:
                        take_weights(t, s, (t + 2) // 2, first)
                        if more:
                            row_rest(t + 1, 1 - s)
                        if not first:
                            results(t - 1, 1 - s)

            row_rest(0, 0)
            tile(0, 0, first=True)
            with dve.Fori(0, (NT - 3) // 2) as i:
                for s2 in range(2):
                    tile(2 * i + (s2 + 1), 1 - s2)
            for t in range(NT - 2, NT):
                tile(t, t % 2, more=t < NT - 1)
            results(NT - 1, (NT - 1) % 2)


_INS = ['x', 'ctx_1024', 'condB_tau', 'fside_BxS2_0', 'L0_xcond_Wq', 'L0_xcond_bq', 'L0_xcond_Wk', 'L0_xcond_bk',
        'L0_xcond_Wv', 'L0_xcond_bv', 'L0_xcond_Wo', 'L0_xcond_bo', 'L0_ffn_gate_w', 'L0_ffn_fc_w', 'L0_ffn_proj_w']


def kernel(**inputs):
    import numpy as _np
    import concourse.bacc as _bacc
    from concourse import mybir as _mybir
    from concourse.bass_utils import run_bass_kernel_spmd as _run

    nc = _bacc.Bacc("TRN2", target_bir_lowering=False, num_devices=1)
    arrays, args = {}, []
    for name in _INS:
        a = _np.ascontiguousarray(inputs[name])
        arrays[f"in_{name}"] = a
        args.append(nc.dram_tensor(f"in_{name}", a.shape, _mybir.dt.from_np(a.dtype), kind="ExternalInput").ap())
    b, s, d = arrays["in_x"].shape
    args.append(nc.dram_tensor("out", (b * s + LIST_PAD, d), F32, kind="ExternalOutput").ap())
    build(nc, *args)
    r = _run(nc, [arrays], core_ids=[0])
    return r.results[0]["out"][:b * s].reshape(b, s, d)
```

```python
from contextlib import ExitStack

import concourse.bass as bass
from concourse import mybir

F32 = mybir.dt.float32
F16 = mybir.dt.float16
BF16 = mybir.dt.bfloat16
I32 = mybir.dt.int32
U32 = mybir.dt.uint32
ALU = mybir.AluOpType
ACT = mybir.ActivationFunctionType
AX = mybir.AxisListType

P = 128
LN_EPS = 1e-5
W_SCALE = 64.0
H = 16
PE_PLAN = dict(first_rows=3, queries=(7, 13), values=((6, 6), (9, 9), (15, 15), (1, 1)), outputs=(4, 5, 6, 6),
               second_rows=10, logits=11, ranks=14)
ACT_PLAN = dict(first_rows=3, queries=(9, 15), second_rows=10, both_rows=15, gap=14)
DVE_PLAN = dict(statistics=1, rstd=1, scale=2, tau=4, divide=((10, 12, 13, 14), (2, 3, 3, 5)), residual=(7, 8),
                rstd2=8, scale2=9, choose=14, notes=15, places=15)
CHUNKS = (1, 1, 0, 1, 0, 1, 1, 1, 2, 1, 2, 0, 2, 0, 2, 1)
AHEAD = 2
LIST_TILE = 256
LIST_PAD = LIST_TILE


class Chain:

    def __init__(self, eng, sem, base=0):
        self.eng, self.sem, self.base, self.n = eng, sem, base, 0

    def __call__(self, ins):
        self.n += 1
        ins.then_inc(self.sem, 1)
        self.eng.wait_ge(self.sem, self.base + self.n)


def settle(eng, passed):
    eng.sem_inc(passed, 1)


def wait(eng, sem, value):
    if not isinstance(value, int) or value > 0:
        eng.wait_ge(sem, value)


def build(nc, x, ctx_in, tau, fside, Wq, bq, Wk, bk, Wv, bv, Wo, bo, gate_w, fc_w, proj_w, out):
    B, S, D = x.shape
    KV = ctx_in.shape[1]
    E, _, F = fc_w.shape
    DK = D // H
    N = B * S
    T = 4
    BLK = T * P
    NBLK = N // BLK
    HALVES = S // BLK
    KD = D // P
    NG = H // 4
    U = NG * T
    CAP = N + LIST_PAD
    NT = (2 * N + E * (LIST_TILE - 1)) // LIST_TILE
    DUMMY = E * CAP
    EARLY = 4
    assert EARLY * LIST_TILE + E * (LIST_TILE - 1) <= 2 * (N - BLK) + LIST_TILE - 1
    ROW = D + 2
    SUB = LIST_TILE // P
    NP = F // (2 * P)
    WE = 2 * KD * F
    MAXT = N // LIST_TILE
    STAGES = 4
    CH = 512
    assert (KD, DK, SUB, F // P, NBLK) == (2, 16, 2, 8, B * HALVES) and 2 * E * 4 * CH == NBLK * U * CH
    assert E * KD * F * 2 == NBLK * U * CH

    lists = nc.dram_tensor("lists", (E * CAP + LIST_TILE, ROW), F32, kind="Internal").ap()

    with ExitStack() as es:
        def sb(name, shape, dt=F32):
            return es.enter_context(nc.sbuf_tensor(name, shape, dt))

        def sem(name):
            return es.enter_context(nc.semaphore(name))

        ps = es.enter_context(nc.psum_tensor("ps", [P, 8, 512], F32))
        SCORE, PROBT, OUTB, SUMB, ODD = [0, 1], [4, 5], 6, 7, [2, 3]
        HID, YB, XB = [0, 1], [4, 5], [6, 7]

        ident = sb("ident", [P, P])
        tri = sb("tri", [P, P], BF16)
        ones_bf = sb("ones_bf", [P, P], BF16)
        head_mask = sb("head_mask", [P, 2, 4])
        iota_e = sb("iota_e", [P, E])
        fcw = sb("fcw", [P, E * WE], F16)
        prw = sb("prw", [P, E * WE], F16)
        gate = sb("gate", [P, KD, E])
        wqT = sb("wqT", [P, KD, D])
        woT = sb("woT", [P, KD, D])
        bq_sb = sb("bq_sb", [P, KD])
        bk_sb = sb("bk_sb", [P, KD])
        bo_sb = sb("bo_sb", [P, D])
        tau4 = sb("tau4", [P, B])
        w_stage = sb("w_stage", [P, STAGES, CH])
        kT = sb("kT", [P, KD, B, KV])
        v = sb("v", [KV, B, D])
        kbd = sb("kbd", [P, KD, 2, 4, KV])
        vpad = sb("vpad", [KV, H, 2 * DK])
        ones_pad = sb("ones_pad", [KV, 2, 2 * DK])
        dparts = sb("dparts", [3, B, KV], BF16)
        tau_cur = sb("tau_cur", [P, 1])
        bq_cur = sb("bq_cur", [P, KD])
        x_in = sb("x_in", [P, T, D])
        x1 = sb("x1", [P, T, D])
        xnT = sb("xnT", [P, 2, KD, BLK])
        qT = sb("qT", [P, KD, BLK])
        attnT = sb("attnT", [P, KD, BLK])
        probs = sb("probs", [P, 4, 4, KV])
        nmax = sb("nmax", [P, 2, 4])
        arena = sb("arena", [P, 4096])
        rows = sb("rows", [P, T, 2, ROW])
        stats = sb("stats", [P, T, 6])
        mv = sb("mv", [P, T, 2])
        ln = sb("ln", [P, 5, T])
        top8 = sb("top8", [P, T, 8])
        top8_at = sb("top8_at", [P, T, 8], U32)
        which = sb("which", [P, 2, T])
        chosen = sb("chosen", [P, 2, T, E])
        chosen_bf = sb("chosen_bf", [P, T, E], BF16)
        place_t = sb("place_t", [P, T, E])
        place = sb("place", [P, E])
        list_base = sb("list_base", [1, E])
        pos = sb("pos", [P, 2, T], I32)
        tw = sb("tw", [P, 4, T])
        row_no = sb("row_no", [P, T])
        tile_row = sb("tile_row", [1, NT], I32)
        tile_w = sb("tile_w", [1, NT], I32)
        pad_at = sb("pad_at", [1, E], I32)

        y_row = sb("y_row", [P, 2, SUB], I32)
        y_scale = sb("y_scale", [P, 2, SUB])

        w_nat = arena[:, 0:2048].rearrange("p (w m d) -> p w m d", w=4, m=KD)
        wkvT = arena[:, 2048:3072].rearrange("p (w k d) -> p w k d", w=2, k=KD)
        ctx_nat = arena[0:KV, 3072:3584].rearrange("p (b d) -> p b d", b=B)
        ctxT = arena[:, 3584:3584 + KD * B * KV].rearrange("p (k n) -> p k n", k=KD)
        bv_sb = rows[0:KV, 0, 0, 0:D]
        d_row = rows[0:1, 1, 0, 0:B * KV]
        d_rest = rows[0:1, 2, :, 0:B * KV]
        d_bf3 = rows[0:1, 3, 0, 0:256].bitcast(BF16)[:, 0:3 * B * KV]
        probsT = arena[0:KV, :].rearrange("p (s j n) -> p s j n", s=2, j=4)
        h16 = arena[:, 0:2048].bitcast(F16).rearrange("p (s c n) -> p s c n", s=4, c=2)
        h32 = arena[:, 2048:3072].rearrange("p (s n) -> p s n", s=2)
        xT16 = arena[:, 3072:4096].bitcast(F16).rearrange("p (s c n) -> p s c n", s=2, c=2)
        halves = [qT[:, :, :].rearrange("p k n -> p (k n)"), xnT[:, 0, :, :].rearrange("p k n -> p (k n)")]
        x_list = [h[:, 0:SUB * ROW].rearrange("p (h r) -> p h r", h=SUB) for h in halves]
        tab_q, tab_x = (h[0:1, SUB * ROW:] for h in halves)
        tab_s = tab_q[:, 0:8 * E].rearrange("p (s e) -> p s e", e=E)
        tab_r = tab_q[:, 8 * E:8 * E + 2 * NT].rearrange("p (r t) -> p r t", r=2)
        tab_jw = tab_q[:, 8 * E + 2 * NT:(8 + MAXT) * E + 2 * NT].rearrange("p (e j) -> p e j", e=E)
        tab_w = [tab_x[:, 0:NT * E], tab_x[:, NT * E:2 * NT * E], tab_q[:, 256:256 + NT * E]]
        tab_w = [w.rearrange("p (t e) -> p t e", e=E) for w in tab_w]
        y = x_in[:, :, :].rearrange("p (s h) d -> p s h d", s=2)
        pad_rows = x1[:, :, :].rearrange("p t d -> p (t d)")[:, 0:SUB * ROW].rearrange("p (h r) -> p h r", h=SUB)
        tab_c = kT[0:1, :, :, :].rearrange("p m b k -> p (m b k)")
        tab_t = tab_c[:, 0:NT * E].rearrange("p (t e) -> p t e", e=E)
        tab_j = tab_c[:, NT * E:(NT + MAXT) * E].rearrange("p (e j) -> p e j", e=E)

        ctx_loaded, w_loaded, b_loaded, f_loaded = sem("ctx_loaded"), sem("w_loaded"), sem("b_loaded"), sem("f_loaded")
        x_loaded = sem("x_loaded")
        stage_loaded = [sem(f"stage_loaded{i}") for i in range(STAGES)]
        out_stored = sem("out_stored")
        consts_ready = sem("consts_ready")
        setup_pe, setup_act, setup_dve = sem("setup_pe"), sem("setup_act"), sem("setup_dve")
        d_split, d_moved = sem("d_split"), sem("d_moved")
        keys_ready, values_ready, x_bias_added = sem("keys_ready"), sem("values_ready"), sem("x_bias_added")
        pool_chain, dve_setup = sem("pool_chain"), sem("dve_setup")
        dve_chain = [sem(f"dve_chain{i}") for i in range(3)]
        hid_high, pool_passed, dve_passed, sp_passed = sem("hid_high"), sem("pool_passed"), sem("dve_passed"), sem("sp_passed")
        xn_ready, tau_ready, res_loaded = sem("xn_ready"), sem("tau_ready"), sem("res_loaded")
        xT_made, xT_copied, q_made, q_ready = sem("xT_made"), sem("xT_copied"), sem("q_made"), sem("q_ready")
        scores_made, shifted, probs_ready = sem("scores_made"), sem("shifted"), sem("probs_ready")
        pT_made, pT_copied, pv_made, attn_ready = sem("pT_made"), sem("pT_copied"), sem("pv_made"), sem("attn_ready")
        o_made, x1_ready = sem("o_made"), sem("x1_ready")
        rows_ready, rows_copied, logits_made = sem("rows_ready"), sem("rows_copied"), sem("logits_made")
        gap_ready, exp_ready, chosen_ready, ranks_made = sem("gap_ready"), sem("exp_ready"), sem("chosen_ready"), sem("ranks_made")
        pos_ready, scattered, rows_free = sem("pos_ready"), sem("scattered"), sem("rows_free")
        w_high, w_rest = sem("w_high"), sem("w_rest")
        tables_ready, pads_written = sem("tables_ready"), sem("pads_written")
        pads_made, ends_ready = sem("pads_made"), sem("ends_ready")
        list_loaded = [sem("list_loaded0"), sem("list_loaded1")]
        lx_made, lx_high, lx_rest = sem("lx_made"), sem("lx_high"), sem("lx_rest")
        hid_made, gelu_ready, hid_split, y_made, y_ready = (
            sem("hid_made"), sem("gelu_ready"), sem("hid_split"), sem("y_made"), sem("y_ready"))
        y_added, taken, adds_before = sem("y_added"), sem("taken"), sem("adds_before")

        def chunks_at(u):
            return range(sum(CHUNKS[:u]), sum(CHUNKS[:u + 1]))

        def stage_dram(e, g, t):
            if g % 2 == 0:
                k, half = divmod(t, 2)
                return fc_w[bass.ds(e, 1), k * P:(k + 1) * P, half * CH:(half + 1) * CH].rearrange("e p n -> p (e n)")
            return proj_w[bass.ds(e, 1), 2 * t * P:(2 * t + 2) * P, :].rearrange("e (h p) n -> p (e h) n", p=P)

        def stage_sb(u, g):
            s = w_stage[:, u % STAGES, :]
            return s if g % 2 == 0 else s.rearrange("p (h n) -> p h n", h=2)

        def split_dst(e, g, t, part):
            if g % 2 == 0:
                k, half = divmod(t, 2)
                return fcw[:, bass.ds(e * WE + (2 * k + part) * F + half * CH, CH)]
            w = prw[:, :].rearrange("p (f c n) -> p f c n", c=2, n=D)
            return w[:, bass.ds(e * (F // P) + 2 * t, 2), part, :]

        def rows_at(t):
            return None if t == NT - 1 else NP - 1 if t == EARLY - 1 else 1

        block = es.enter_context(nc.Block())

        @block.sync
        def _(sp):
            x_rows = x.rearrange("b s d -> (b s) d")
            sp.dma_start(x_in[:], x_rows[0:BLK, :].rearrange("(t p) d -> p t d", p=P)).then_inc(x_loaded, 16)
            for i, w in enumerate((Wk, Wv, Wq, Wo)):
                sp.dma_start(w_nat[:, i], w.rearrange("(m p) d -> p m d", p=P)).then_inc(w_loaded, 16)
            sp.dma_start(ctx_nat, ctx_in.rearrange("b k d -> k b d")).then_inc(ctx_loaded, 16)
            sp.dma_start(d_row, fside.rearrange("(a b) k -> a (b k)", a=1)).then_inc(f_loaded, 16)
            sp.dma_start(bk_sb[:], bk.rearrange("(m p) -> p m", p=P), allow_slow_non_contiguous=True).then_inc(b_loaded, 16)
            sp.dma_start(bq_sb[:], bq.rearrange("(m p) -> p m", p=P), allow_slow_non_contiguous=True).then_inc(b_loaded, 16)
            sp.dma_start(bv_sb, bv.rearrange("(a d) -> a d", a=1).to_broadcast([KV, D])).then_inc(b_loaded, 16)
            sp.dma_start(bo_sb[:], bo.rearrange("(a d) -> a d", a=1).to_broadcast([P, D])).then_inc(b_loaded, 16)
            sp.dma_start(tau4[:], tau.rearrange("(a b) -> a b", a=1).to_broadcast([P, B])).then_inc(b_loaded, 16)
            sp.dma_start(gate[:], gate_w.rearrange("(k p) e -> p k e", p=P)).then_inc(b_loaded, 16)
            sp.wait_ge(consts_ready, 1)
            sp.dma_start(out[N:N + LIST_PAD, :].rearrange("(h p) d -> p h d", p=P), pad_rows[:, :, 0:D]).then_inc(out_stored, 16)
            sp.dma_start(lists[DUMMY:DUMMY + LIST_TILE, :].rearrange("(h p) r -> p h r", p=P), pad_rows[:]).then_inc(pads_written, 16)

            def load_block(dst, k, loaded):
                sp.dma_start(dst[:], x_rows[bass.ds(k * BLK, BLK), :].rearrange("(t p) d -> p t d", p=P)).then_inc(loaded, 16)

            def store_x1(k):
                sp.wait_ge(x1_ready, k + 1)
                sp.dma_start(out[bass.ds(k * BLK, BLK), :].rearrange("(t p) d -> p t d", p=P), x1[:]).then_inc(out_stored, 16)

            def body(k, post=True, pre=True):
                def load_next():
                    sp.wait_ge(q_made, KD * k + 1)
                    load_block(x_in, k + 1, x_loaded)

                if pre and post:
                    load_next()
                for c in range(U):
                    g, t = divmod(c, T)
                    wait(sp, w_rest, U * k + c + 1 - STAGES)
                    sp.dma_start(stage_sb(c, g), stage_dram(2 * k + g // 2, g, t)).then_inc(stage_loaded[c % STAGES], 16)
                    if pre and not post and c == STAGES - 1:
                        load_next()
                    if post and c == 0:
                        if not isinstance(k, int):
                            sp.wait_ge(pads_written, 16)
                        sp.wait_ge(q_made, KD * (k + 1))
                        settle(sp, sp_passed)
                        sp.wait_ge(out_stored, 16 * k)
                        load_block(x1, k - 1, res_loaded)
                    if post and c == 8:
                        store_x1(k - 1)

            body(0, post=False)
            with sp.Fori(1, NBLK - 1) as k:
                body(k)
            body(NBLK - 1, pre=False)
            sp.wait_ge(rows_ready, NBLK - 1)
            sp.wait_ge(out_stored, 16 * NBLK)
            load_block(x1, NBLK - 1, res_loaded)

            def load_tile(t, slot):
                at = sp.value_load(tile_row[0:1, bass.ds(t, 1)], min_val=0, max_val=DUMMY)
                sp.dma_start(x_list[slot], lists[bass.ds(at, LIST_TILE), :].rearrange("(h p) r -> p h r", p=P)).then_inc(list_loaded[slot], 16)

            def load_next_tile(t, slot):
                sp.wait_ge(lx_made, t - 1)
                sp.wait_ge(taken, t - 1)
                load_tile(t, slot)

            sp.wait_ge(tables_ready, 1)
            sp.wait_ge(pv_made, NG * NBLK)
            sp.wait_ge(scattered, 16 * 2 * T * (NBLK - 1))
            for t in range(2):
                load_tile(t, t)
            store_x1(NBLK - 1)
            for t in range(2, EARLY):
                load_next_tile(t, t % 2)
            sp.wait_ge(ends_ready, 1)
            sp.wait_ge(pads_made, 1)
            for e in range(E):
                at = sp.value_load(pad_at[0:1, e:e + 1], min_val=e * CAP, max_val=e * CAP + N)
                sp.dma_start(lists[bass.ds(at, LIST_PAD), :].rearrange("(h p) r -> p h r", p=P), pad_rows[:]).then_inc(pads_written, 16)
            sp.wait_ge(tables_ready, 2)
            sp.wait_ge(pads_written, 16 * (E + 1))
            sp.wait_ge(scattered, 16 * 2 * T * NBLK)
            with sp.Fori(0, (NT - EARLY) // 2) as i:
                for s in range(2):
                    load_next_tile(2 * i + (s + EARLY), (s + EARLY) % 2)
            for t in range(EARLY + (NT - EARLY) // 2 * 2, NT):
                load_next_tile(t, t % 2)
            sp.wait_ge(out_stored, 16 * (NBLK + 1))
            sp.wait_ge(y_added, 16 * SUB * NT)

        @block.gpsimd
        def _(pool):
            link = Chain(pool, pool_chain)

            def make_pads():
                link(pool.memset(pad_rows[:], 0.0))
                link(pool.iota(pad_rows[:, :, D + 1:D + 2].bitcast(I32), pattern=[[P, SUB], [0, 1]], base=N, channel_multiplier=1))

            make_pads()
            link(pool.memset(ident[:], 0.0))
            link(pool.affine_select(out=ident[:], in_=ident[:], compare_op=ALU.not_equal, fill=1.0, base=0,
                                    pattern=[[-1, P]], channel_multiplier=1))
            pool.sem_inc(consts_ready, 1)
            link(pool.memset(ones_bf[:], 1.0))
            link(pool.memset(tri[:], 1.0))
            link(pool.affine_select(out=tri[:], in_=tri[:], compare_op=ALU.is_gt, fill=0.0, base=0,
                                    pattern=[[1, P]], channel_multiplier=-1))
            link(pool.memset(head_mask[:], 1.0))
            link(pool.affine_select(out=head_mask[:], in_=head_mask[:], compare_op=ALU.is_ge, fill=0.0, base=0,
                                    pattern=[[-DK, 2], [-2 * DK, 4]], channel_multiplier=1))
            link(pool.affine_select(out=head_mask[:], in_=head_mask[:], compare_op=ALU.is_ge, fill=0.0, base=DK - 1,
                                    pattern=[[DK, 2], [2 * DK, 4]], channel_multiplier=-1))
            for dst, base_step in ((iota_e, 1), (place, CAP), (list_base, CAP)):
                link(pool.iota(dst[:], pattern=[[base_step, E]], base=0, channel_multiplier=0, allow_small_or_imprecise_dtypes=True))
            link(pool.iota(row_no[:], pattern=[[P, T]], base=0, channel_multiplier=1, allow_small_or_imprecise_dtypes=True))
            link(pool.memset(ones_pad[:], 0.0))
            link(pool.memset(vpad[:], 0.0))
            for par in range(2):
                link(pool.memset(ones_pad[:, par, par * DK:(par + 1) * DK], 1.0))
            pool.sem_inc(consts_ready, 1)
            def batch_keys(b, m):
                wait(pool, scores_made, U * HALVES * b - (0 if m or not b else U // 2))
                pool.tensor_tensor(kbd[:, m].rearrange("p a j k -> p (a j) k"),
                                   kT[:, m, b:b + 1, :].to_broadcast([P, 8, KV]),
                                   head_mask[:].rearrange("p a (j o) -> p (a j) o", o=1).to_broadcast([P, 8, KV]), ALU.mult).then_inc(keys_ready, 1)

            def batch_values(b):
                wait(pool, pv_made, NG * HALVES * b)
                for par in range(2):
                    last = pool.tensor_copy(vpad[:, par::2, par * DK:(par + 1) * DK],
                                            v[:, b, :].rearrange("p (h d) -> p h d", h=H)[:, par::2, :])
                last.then_inc(values_ready, 1)

            def weight_rest(k, c):
                g, t = divmod(c, T)
                pool.wait_ge(w_high, U * k + c + 1)
                pool.tensor_tensor(split_dst(2 * k + g // 2, g, t, 1), stage_sb(c, g), split_dst(2 * k + g // 2, g, t, 0), ALU.subtract).then_inc(w_rest, 1)

            def residual_bias(k):
                pool.wait_ge(res_loaded, 16 * (k + 1))
                pool.tensor_tensor(x1[:], x1[:], bo_sb[:].rearrange("p (o d) -> p o d", o=1).to_broadcast([P, T, D]), ALU.add).then_inc(x_bias_added, 1)

            def scatter(k):
                pool.wait_ge(rows_copied, k + 1)
                pool.wait_ge(pos_ready, k + 1)
                settle(pool, pool_passed)
                for s in range(2):
                    for t in range(T):
                        pool.indirect_dma_start(lists[:, :], bass.IndirectOffsetOnAxis(ap=pos[:, s, t:t + 1], axis=0),
                                                rows[:, t, s, :], None).then_inc(scattered, 16)

            def free_rows(k):
                pool.wait_ge(scattered, 16 * 2 * T * (k + 1))
                pool.sem_inc(rows_free, 1)

            for m in range(KD):
                pool.wait_ge(setup_act, 6 + m)
                batch_keys(0, m)
            pool.wait_ge(d_moved, 48)
            pool.wait_ge(setup_dve, B)
            pool.sem_inc(rows_free, 1)
            batch_values(0)
            for k in range(NBLK):
                if k >= 2:
                    scatter(k - 2)
                if k and k % HALVES == 0:
                    batch_keys(k // HALVES, 1)
                    batch_values(k // HALVES)
                    if k // HALVES == B - 1:
                        pool.wait_ge(keys_ready, KD * B)
                        link(pool.iota(tab_j[:], pattern=[[0, E], [LIST_TILE, MAXT]], base=0, channel_multiplier=0, allow_small_or_imprecise_dtypes=True))
                        link(pool.iota(tab_t[:], pattern=[[1, NT], [0, E]], base=0, channel_multiplier=0, allow_small_or_imprecise_dtypes=True))
                for c in range(U):
                    if c == U - 2 and k == NBLK - 1:
                        residual_bias(k)
                        scatter(k - 1)
                    weight_rest(k, c)
                    if c == 2 and k >= 1:
                        residual_bias(k - 1)
                    if c == 4 and k >= 2:
                        free_rows(k - 2)
                    if c == 6 and (k + 1) % HALVES == 0 and k + 1 < NBLK:
                        batch_keys((k + 1) // HALVES, 0)
            free_rows(NBLK - 2)
            pool.wait_ge(rows_ready, NBLK)
            pool.wait_ge(out_stored, 16 * (NBLK + 1))
            make_pads()
            pool.sem_inc(pads_made, 1)
            scatter(NBLK - 1)

            def add_tile(t, s, first=False):
                if not first:
                    pool.wait_ge(y_added, 16 * SUB * t)
                pool.sem_inc(adds_before, 1)
                pool.wait_ge(y_ready, t + 1)
                settle(pool, pool_passed)
                for h in range(SUB):
                    pool.indirect_dma_start(out[:, :], bass.IndirectOffsetOnAxis(ap=y_row[:, s, h:h + 1], axis=0),
                                            y[:, s, h, :], None, compute_op=ALU.add).then_inc(y_added, 16)

            add_tile(0, 0, first=True)
            with pool.Fori(0, (NT - 1) // 2) as i:
                for s2 in range(2):
                    add_tile(2 * i + s2 + 1, (s2 + 1) % 2)
            pool.wait_ge(y_added, 16 * SUB * NT)

        @block.tensor
        def _(pe):
            pe.wait_ge(consts_ready, 1)
            pe.wait_ge(w_loaded, 64)
            for w in range(4):
                for k in range(KD):
                    for m in range(KD):
                        last = pe.transpose(ps[:, w, k * D + m * P:k * D + (m + 1) * P], w_nat[:, w, m, k * P:(k + 1) * P], ident[:])
                last.then_inc(setup_pe, 1)
            pe.wait_ge(ctx_loaded, 16)
            for k in range(KD):
                for b in range(B):
                    last = pe.transpose(ps[:, 4, (k * B + b) * KV:(k * B + b + 1) * KV], ctx_nat[:, b, k * P:(k + 1) * P], ident[0:KV, 0:KV])
            last.then_inc(setup_pe, 1)

            def transposed(src, n):
                for c in range(KD):
                    for t in range(T):
                        last = pe.transpose(ps[:, ODD[c], t * P:(t + 1) * P], src[:, t, c * P:(c + 1) * P], ident[:])
                    last.then_inc(xT_made, 1)

            def first_rows(k, n):
                pe.wait_ge(xn_ready, k + 1)
                transposed(x_in, n)

            pe.wait_ge(setup_act, 4)
            first_rows(0, 1)
            pe.wait_ge(setup_act, 5)
            for m in range(KD):
                for k in range(KD):
                    last = pe.matmul(ps[:, 5 + m, 0:B * KV], wkvT[:, 0, k, m * P:(m + 1) * P], ctxT[:, k, :], start=(k == 0), stop=(k == KD - 1))
                last.then_inc(setup_pe, 1)
            for b in range(B):
                for k in range(KD):
                    last = pe.matmul(ps[0:KV, 7 if b else 4, 0:D], ctxT[:, k, b * KV:(b + 1) * KV], wkvT[:, 1, k, :], start=(k == 0), stop=(k == KD - 1))
                last.then_inc(setup_pe, 1)
            pe.wait_ge(consts_ready, 2)

            def project_queries(m, n):
                pe.wait_ge(xT_copied, KD * n)
                for c in range(KD):
                    last = pe.matmul(ps[:, ODD[m], :], wqT[:, c, m * P:(m + 1) * P], xnT[:, 0, c, :], start=(c == 0), stop=(c == KD - 1))
                last.then_inc(q_made, 1)

            def scores(k, u):
                g, t = divmod(u, T)
                m, par = divmod(g, 2)
                if u % (U // 2) == 0:
                    pe.wait_ge(q_ready, KD * k + m + 1)
                    pe.wait_ge(keys_ready, KD * (k // HALVES) + m + 1)
                wait(pe, shifted, U * k + u - 1)
                o = ps[:, SCORE[u % 2], 0:4 * KV]
                pe.matmul(o, qT[:, m, t * P:(t + 1) * P], kbd[:, m, par].rearrange("p j k -> p (j k)"), start=True, stop=False)
                pe.matmul(o, ones_bf[0:3, :], dparts[:, bass.ds(k // HALVES, 1), :].to_broadcast([3, 4, KV]), start=False, stop=True).then_inc(scores_made, 1)

            def transpose_probs(k, u):
                pe.wait_ge(probs_ready, U * k + u + 1)
                wait(pe, pT_copied, U * k + u - 1)
                for j in range(4):
                    last = pe.transpose(ps[0:KV, PROBT[u % 2], j * P:(j + 1) * P], probs[:, u % 4, j, :], ident[:])
                last.then_inc(pT_made, 1)

            def weigh_values(k, g, u=None):
                m, par = divmod(g, 2)
                parts = [part for part in range(2) if u in (None, PE_PLAN["values"][g][part])]
                if 0 in parts:
                    pe.wait_ge(pT_copied, U * k + T * (g + 1))
                    if g == 0:
                        pe.wait_ge(values_ready, k // HALVES + 1)
                    if par == 0:
                        wait(pe, attn_ready, T * (KD * k + m))
                for part in parts:
                    for j in range(4):
                        last = pe.matmul(ps[2 * DK * j:2 * DK * (j + 1), (OUTB, SUMB)[part], :],
                                         ones_pad[:, par, :] if part else vpad[:, 8 * m + 2 * j + par, :],
                                         probsT[:, g % 2, j, :], start=(par == 0), stop=(par == 1))
                if 1 in parts:
                    last.then_inc(pv_made, 1)

            def project_outputs(k, t):
                pe.wait_ge(attn_ready, T * (KD * k + 1) + t + 1)
                for m in range(KD):
                    last = pe.matmul(ps[:, ODD[t // 2], (t % 2) * D:(t % 2 + 1) * D], attnT[:, m, t * P:(t + 1) * P], woT[:, m, :],
                                     start=(m == 0), stop=(m == KD - 1))
                if t % 2:
                    last.then_inc(o_made, 1)

            def second_rows(k, n):
                pe.wait_ge(rows_ready, k + 1)
                transposed(rows[:, :, 0, :], n)

            def logits(n):
                pe.wait_ge(xT_copied, KD * n)
                for t in range(T):
                    for c in range(KD):
                        last = pe.matmul(ps[:, ODD[0], t * E:(t + 1) * E], xnT[:, 1, c, t * P:(t + 1) * P], gate[:, c, :], start=(c == 0), stop=(c == KD - 1))
                last.then_inc(logits_made, 1)

            def ranks(k):
                pe.wait_ge(chosen_ready, k + 1)
                pe.matmul(ps[:, ODD[0], 0:T * E], tri[:], chosen_bf[:].rearrange("p t e -> p (t e)"), start=True, stop=False, skip_group_check=True)
                for t in range(T - 1):
                    later = T - 1 - t
                    pe.matmul(ps[:, ODD[0], (t + 1) * E:T * E].rearrange("p (t e) -> p t e", e=E), ones_bf[:],
                              chosen_bf[:, t:t + 1, :].to_broadcast([P, later, E]), start=False, stop=(t == T - 2), skip_group_check=True)
                for t in range(T):
                    last = pe.matmul(ps[:, ODD[0], T * E:(T + 1) * E], ones_bf[:], chosen_bf[:, t, :], start=(t == 0), stop=(t == T - 1),
                                     skip_group_check=True)
                last.then_inc(ranks_made, 1)

            def body(k, post=True, pre=True):
                n_first, n_second = (2 * k + 1 if post else 2), (2 * k + 2 if pre else 2 * k + 1)
                if not post:
                    pe.wait_ge(d_moved, 48)
                    pe.wait_ge(setup_dve, B)
                    scores(k, 0)
                    scores(k, 1)
                for u in range(U):
                    if u + 2 < U:
                        scores(k, u + 2)
                    elif pre:
                        scores(k + 1, u + 2 - U)
                    if u >= 1:
                        transpose_probs(k, u - 1)
                    elif post:
                        transpose_probs(k - 1, U - 1)
                    if post:
                        weigh_values(k - 1, NG - 1, u)
                    if not post and u == 0:
                        project_queries(1, 1)
                    if not post and u == PE_PLAN["first_rows"]:
                        pe.wait_ge(q_ready, KD)
                    if pre and u == PE_PLAN["first_rows"]:
                        first_rows(k + 1, n_first)
                    if post and u == PE_PLAN["outputs"][0]:
                        if pre:
                            pe.wait_ge(xT_copied, KD * n_first)
                        else:
                            pe.wait_ge(pos_ready, k - 1)
                    for t in range(T):
                        if post and u == PE_PLAN["outputs"][t]:
                            project_outputs(k - 1, t)
                    weigh_values(k, 0, u)
                    if pre and u == PE_PLAN["queries"][0]:
                        if post:
                            pe.wait_ge(x1_ready, k)
                        project_queries(0, n_first)
                    weigh_values(k, 1, u)
                    if post and u == PE_PLAN["second_rows"]:
                        if pre:
                            pe.wait_ge(q_ready, KD * (k + 1) + 1)
                        second_rows(k - 1, n_second)
                    if post and u == PE_PLAN["logits"]:
                        logits(n_second)
                    if post and u == PE_PLAN["ranks"]:
                        ranks(k - 1)
                    if pre and u == PE_PLAN["queries"][1]:
                        project_queries(1, n_first)
                    weigh_values(k, 2, u)

            project_queries(0, 1)
            body(0, post=False)
            with pe.Fori(1, NBLK - 1) as k:
                body(k)
            body(NBLK - 1, pre=False)
            transpose_probs(NBLK - 1, U - 1)
            weigh_values(NBLK - 1, NG - 1)
            pe.wait_ge(pos_ready, NBLK - 1)
            for t in range(T):
                project_outputs(NBLK - 1, t)

            among = {0: {1: lambda: second_rows(NBLK - 1, 2 * NBLK), 3: lambda: logits(2 * NBLK)},
                     1: {0: lambda: ranks(NBLK - 1)}}
            pe.wait_ge(tables_ready, 1)
            pe.wait_ge(w_high, NBLK * U)
            pe.wait_ge(w_rest, NBLK * U)

            def list_rows(t, s, n):
                pe.wait_ge(list_loaded[s], 16 * n)
                for k in range(KD):
                    for h in range(SUB):
                        last = pe.transpose(ps[:, XB[s], (k * SUB + h) * P:(k * SUB + h + 1) * P], x_list[s][:, h, k * P:(k + 1) * P], ident[:])
                last.then_inc(lx_made, 1)

            def hidden(t, s, step, w):
                if step == 0:
                    pe.wait_ge(lx_rest, t + 1)
                wait(pe, gelu_ready, NP * t + step - 1)
                for f2 in range(2):
                    f = 2 * step + f2
                    o = ps[:, HID[step % 2], f2 * LIST_TILE:(f2 + 1) * LIST_TILE]
                    n = 0
                    for k in range(KD):
                        for wp, xp in ((0, 0), (0, 1), (1, 0)):
                            last = pe.matmul(o, fcw[:, bass.ds(w + ((2 * k + wp) * F + f * P), P)],
                                             xT16[:, s, xp, k * LIST_TILE:(k + 1) * LIST_TILE], start=(n == 0), stop=(n == 3 * KD - 1))
                            n += 1
                last.then_inc(hid_made, 1)

            def outputs(t, s, step, w):
                pe.wait_ge(hid_split, NP * t + step + 1)
                for f2 in range(2):
                    for wp, hp in ((0, 0), (0, 1), (1, 0)):
                        for h in range(SUB):
                            first = (step, f2, wp, hp, h) == (0, 0, 0, 0, 0)
                            final = (step, f2, wp) == (NP - 1, 1, 1)
                            last = pe.matmul(ps[:, YB[s], h * D:(h + 1) * D],
                                             h16[:, step, hp, f2 * LIST_TILE + h * P:f2 * LIST_TILE + (h + 1) * P],
                                             prw[:, bass.ds(w + (2 * (2 * step + f2) + wp) * D, D)],
                                             start=first, stop=final, skip_group_check=True)
                if step == NP - 1:
                    last.then_inc(y_made, 1)

            def weights_of(t):
                return pe.value_load(tile_w[0:1, bass.ds(t, 1)], min_val=0, max_val=(E - 1) * WE)

            LAG = 2

            def tile(t, s, w_last, rows_at=1, among={}):
                w = weights_of(t)
                for step in range(NP):
                    hidden(t, s, step, w)
                    if step == rows_at:
                        list_rows(t + 1, 1 - s, (t + 3) // 2)
                    if step >= LAG:
                        outputs(t, s, step - LAG, w)
                    elif w_last is not None:
                        outputs(t - 1, 1 - s, NP - LAG + step, w_last)
                    if step in among:
                        among[step]()

            list_rows(0, 0, 1)
            for t in range(EARLY):
                tile(t, t % 2, weights_of(t - 1) if t else None, rows_at(t), among.get(t, {}))
            pe.wait_ge(tables_ready, 2)
            with pe.Fori(0, (NT - EARLY - 2) // 2) as i:
                for s2 in range(2):
                    t = 2 * i + (s2 + EARLY)
                    tile(t, (s2 + EARLY) % 2, weights_of(t - 1))
            for t in range(EARLY + (NT - EARLY - 2) // 2 * 2, NT):
                tile(t, t % 2, weights_of(t - 1), rows_at(t))
            w = weights_of(NT - 1)
            for step in range(NP - LAG, NP):
                outputs(NT - 1, (NT - 1) % 2, step, w)

        @block.scalar
        def _(act):
            for i, dst in enumerate((wkvT[:, 0], wkvT[:, 1], wqT[:], woT[:])):
                act.wait_ge(setup_pe, i + 1)
                act.copy(dst, ps[:, i, :].rearrange("p (k d) -> p k d", k=KD)).then_inc(setup_act, 1)
            act.wait_ge(setup_pe, 5)
            act.copy(ctxT, ps[:, 4, 0:KD * B * KV].rearrange("p (k n) -> p k n", k=KD)).then_inc(setup_act, 1)
            def copy_rows(n, second):
                for c in range(KD):
                    act.wait_ge(xT_made, KD * (n - 1) + c + 1)
                    act.copy(xnT[:, second, c, :], ps[:, ODD[c], :]).then_inc(xT_copied, 1)

            copy_rows(1, 0)
            act.wait_ge(b_loaded, 96)
            for m in range(KD):
                act.wait_ge(setup_pe, 6 + m)
                act.activation(kT[:, m].rearrange("p b k -> p (b k)"), ps[:, 5 + m, 0:B * KV], ACT.Identity, bias=bk_sb[:, m:m + 1]).then_inc(setup_act, 1)
            for i in range(3):
                act.wait_ge(d_split, 1)
                act.dma_start(dparts[i:i + 1, :, :].rearrange("p b k -> p (b k)"), d_bf3[:, i * B * KV:(i + 1) * B * KV]).then_inc(d_moved, 16)

            def copy_queries(k, m):
                if m == 0:
                    act.wait_ge(tau_ready, k + 1)
                act.wait_ge(q_made, KD * k + m + 1)
                act.activation(qT[:, m, :], ps[:, ODD[m], :], ACT.Identity, bias=bq_cur[:, m:m + 1], scale=tau_cur[:, 0:1]).then_inc(q_ready, 1)

            def exponentials(k, u):
                act.wait_ge(shifted, U * k + u + 1)
                act.activation(probs[:, u % 4], probs[:, u % 4], ACT.Exp).then_inc(probs_ready, 1)

            def copy_probs(k, u):
                act.wait_ge(pT_made, U * k + u + 1)
                g, t = divmod(u, T)
                if t == 0:
                    wait(act, pv_made, NG * k + g - 1)
                act.copy(probsT[:, g % 2, :, t * P:(t + 1) * P], ps[0:KV, PROBT[u % 2], :].rearrange("p (j n) -> p j n", j=4)).then_inc(pT_copied, 1)

            def weight_high(k, c):
                g, t = divmod(c, T)
                act.wait_ge(stage_loaded[c % STAGES], 16 * (U // STAGES * k + c // STAGES + 1))
                act.activation(split_dst(2 * k + g // 2, g, t, 0), stage_sb(c, g), ACT.Copy, scale=W_SCALE)
                act.activation(w_stage[:, c % STAGES, :], w_stage[:, c % STAGES, :], ACT.Copy, scale=W_SCALE).then_inc(w_high, 1)

            def both_rows(k):
                act.wait_ge(rows_ready, k + 1)
                act.copy(rows[:, :, 1, 0:D], rows[:, :, 0, 0:D]).then_inc(rows_copied, 1)

            def gap_exponential(k):
                act.wait_ge(gap_ready, k + 1)
                act.activation(tw[:, 1, :], tw[:, 0, :], ACT.Exp).then_inc(exp_ready, 1)

            def body(k, post=True, pre=True):
                n_first, n_second = (2 * k + 1 if post else 2), (2 * k + 2 if pre else 2 * k + 1)
                for u in range(U):
                    exponentials(k, u)
                    if u >= 2:
                        copy_probs(k, u - 2)
                    elif post:
                        copy_probs(k - 1, U + u - 2)
                    if not post and u == 0:
                        copy_queries(0, 1)
                    for c in chunks_at(u):
                        if post or c >= AHEAD:
                            weight_high(k, c)
                    if pre and u == ACT_PLAN["first_rows"]:
                        copy_rows(n_first, 0)
                    if pre and u == ACT_PLAN["queries"][0]:
                        copy_queries(k + 1, 0)
                    if post and u == ACT_PLAN["second_rows"]:
                        copy_rows(n_second, 1)
                    if post and u == ACT_PLAN["both_rows"]:
                        both_rows(k - 1)
                    if post and u == ACT_PLAN["gap"]:
                        gap_exponential(k - 1)
                    if pre and u == ACT_PLAN["queries"][1]:
                        copy_queries(k + 1, 1)

            for c in range(AHEAD):
                weight_high(0, c)
            copy_queries(0, 0)
            body(0, post=False)
            with act.Fori(1, NBLK - 1) as k:
                body(k)
            body(NBLK - 1, pre=False)
            for u in (U - 2, U - 1):
                copy_probs(NBLK - 1, u)

            def routed_rows():
                copy_rows(2 * NBLK, 1)
                both_rows(NBLK - 1)

            among = {0: {1: routed_rows, 3: lambda: gap_exponential(NBLK - 1)}}
            def row_high(t, s):
                act.wait_ge(lx_made, t + 1)
                act.copy(xT16[:, s, 0, :], ps[:, XB[s], :]).then_inc(lx_high, 1)

            def gelu(t, step):
                act.wait_ge(hid_made, NP * t + step + 1)
                wait(act, hid_split, NP * t + step - 1)
                act.activation(h32[:, step % 2, :], ps[:, HID[step % 2], :], ACT.Gelu, scale=1.0 / W_SCALE).then_inc(gelu_ready, 1)

            def tile(t, s, rows_at=1, among={}):
                for step in range(NP):
                    gelu(t, step)
                    if step == rows_at:
                        row_high(t + 1, 1 - s)
                    if step in among:
                        among[step]()

            row_high(0, 0)
            for t in range(EARLY):
                tile(t, t % 2, rows_at(t), among.get(t, {}))
            with act.Fori(0, (NT - EARLY - 2) // 2) as i:
                for s2 in range(2):
                    tile(2 * i + (s2 + EARLY), (s2 + EARLY) % 2)
            for t in range(EARLY + (NT - EARLY - 2) // 2 * 2, NT):
                tile(t, t % 2, rows_at(t))

        @block.vector
        def _(dve):
            DVE_CHAIN = 66

            def rows_norm(src, dst):
                def statistics(ts=range(T)):
                    for t in ts:
                        last = dve.bn_stats(stats[:, t, :], src[:, t, :])
                    link(last)
                    if T - 1 in ts:
                        settle(dve, dve_passed)
                        for t in range(T):
                            last = dve.bn_aggr(mv[:, t, :], stats[:, t, :])
                        link(last)

                def rstd():
                    var, half_bits, r, a, b = (ln[:, i, :] for i in range(5))
                    link(dve.tensor_scalar(var, mv[:, :, 1], LN_EPS, None, ALU.add))
                    link(dve.tensor_scalar(half_bits.bitcast(I32), var.bitcast(I32), 1, None, ALU.logical_shift_right))
                    link(dve.tensor_scalar(r.bitcast(I32), half_bits.bitcast(I32), -1.0, float(0x5F3759DF), ALU.mult, ALU.add))
                    for _ in range(3):
                        link(dve.scalar_tensor_tensor(out=a, in0=var, scalar=-0.5, in1=r, op0=ALU.mult, op1=ALU.mult))
                        link(dve.tensor_tensor(b, a, r, ALU.mult))
                        link(dve.scalar_tensor_tensor(out=r, in0=b, scalar=1.5, in1=r, op0=ALU.add, op1=ALU.mult))

                def scale(ready):
                    for t in range(T):
                        last = dve.tensor_scalar(dst(t), src[:, t, :], mv[:, t, 0:1], ln[:, 2, t:t + 1], ALU.subtract, ALU.mult)
                    last.then_inc(ready, 1)

                return statistics, rstd, scale

            statistics1, rstd1, scale1 = rows_norm(x_in, lambda t: x_in[:, t, :])
            statistics2, rstd2, scale2 = rows_norm(x1, lambda t: rows[:, t, 0, 0:D])

            def tau_of(k):
                wait(dve, q_ready, KD * k)
                link(dve.tensor_scalar(tau_cur[:], tau4[:, bass.ds(k // HALVES, 1)], 0.25, None, ALU.mult))
                dve.tensor_scalar(bq_cur[:], bq_sb[:], tau_cur[:, 0:1], None, ALU.mult).then_inc(tau_ready, 1)

            def shifted_scores(k, u):
                s = ps[:, SCORE[u % 2], 0:4 * KV].rearrange("p (j k) -> p j k", j=4)
                dve.wait_ge(scores_made, U * k + u + 1)
                link(dve.tensor_reduce(nmax[:, u % 2, :], s, AX.X, ALU.max, negate=True))
                wait(dve, pT_made, U * k + u - 3)
                dve.tensor_tensor(probs[:, u % 4], s, nmax[:, u % 2, :].rearrange("p (j o) -> p j o", o=1).to_broadcast([P, 4, KV]), ALU.add).then_inc(shifted, 1)

            def divide(k, m, t):
                dve.wait_ge(pv_made, NG * k + 2 * m + 2)
                n = slice(t * P, (t + 1) * P)
                link(dve.reciprocal(attnT[:, m, n], ps[:, SUMB, n]))
                dve.tensor_tensor(attnT[:, m, n], ps[:, OUTB, n], attnT[:, m, n], ALU.mult).then_inc(attn_ready, 1)

            def residual(k, i):
                if i == 0:
                    dve.wait_ge(x_bias_added, k + 1)
                dve.wait_ge(o_made, 2 * k + i + 1)
                ts = range(2 * i, 2 * i + 2)
                link(dve.tensor_tensor(x1[:, 2 * i:2 * i + 2, :], ps[:, ODD[i], :].rearrange("p (t d) -> p t d", t=2), x1[:, 2 * i:2 * i + 2, :], ALU.add))
                if i == 1:
                    dve.sem_inc(x1_ready, 1)
                    settle(dve, dve_passed)
                statistics2(ts)

            def choose(k):
                dve.wait_ge(logits_made, k + 1)
                settle(dve, dve_passed)
                lg = ps[:, ODD[0], 0:T * E].rearrange("p (t e) -> p t e", t=T)
                for t in range(T):
                    last = dve.max(top8[:, t, :], lg[:, t, :])
                link(last)
                settle(dve, dve_passed)
                for t in range(T):
                    last = dve.max_index(top8_at[:, t, :], top8[:, t, :], lg[:, t, :])
                link(last)
                dve.tensor_tensor(tw[:, 0, :], top8[:, :, 1], top8[:, :, 0], ALU.subtract).then_inc(gap_ready, 1)
                link(dve.tensor_copy(which[:].rearrange("p s t -> p t s"), top8_at[:, :, 0:2]))
                for s in range(2):
                    last = dve.tensor_tensor(chosen[:, s], which[:, s, :].rearrange("p (t o) -> p t o", o=1).to_broadcast([P, T, E]),
                                             iota_e[:].rearrange("p (o e) -> p o e", o=1).to_broadcast([P, T, E]), ALU.is_equal)
                link(last)
                dve.tensor_tensor(chosen_bf[:], chosen[:, 0], chosen[:, 1], ALU.add).then_inc(chosen_ready, 1)

            def row_notes(k):
                dve.wait_ge(exp_ready, k + 1)
                link(dve.tensor_scalar(tw[:, 2, :], tw[:, 1, :], 1.0, None, ALU.add))
                link(dve.reciprocal(tw[:, 3, :], tw[:, 2, :]))
                dve.tensor_copy(rows[:, :, 0, D], tw[:, 3, :])
                dve.tensor_tensor(rows[:, :, 1, D], tw[:, 1, :], tw[:, 3, :], ALU.mult)
                for s in range(2):
                    last = dve.tensor_copy(rows[:, :, s, D + 1].bitcast(I32), row_no[:])
                link(last)
                dve.tensor_scalar(row_no[:], row_no[:], float(BLK), None, ALU.add)

            def places(k):
                dve.wait_ge(ranks_made, k + 1)
                link(dve.tensor_tensor(place_t[:], ps[:, ODD[0], 0:T * E].rearrange("p (t e) -> p t e", t=T),
                                       place[:].rearrange("p (o e) -> p o e", o=1).to_broadcast([P, T, E]), ALU.add))
                dve.tensor_tensor(place[:], ps[:, ODD[0], T * E:(T + 1) * E], place[:], ALU.add)
                for s in range(2):
                    last = dve.tensor_tensor(chosen[:, s], chosen[:, s], place_t[:], ALU.mult)
                link(last)
                for s in range(2):
                    last = dve.tensor_reduce(which[:, s, :], chosen[:, s], AX.X, ALU.add)
                link(last)
                dve.tensor_copy(pos[:], which[:]).then_inc(pos_ready, 1)

            def scale_rows(k):
                dve.wait_ge(rows_free, k + 1)
                scale2(rows_ready)

            def body(k, post=True, pre=True):
                after = {u: [] for u in range(U)}
                plan = DVE_PLAN
                if pre:
                    after[plan["statistics"]] += [lambda: dve.wait_ge(x_loaded, 16 * (k + 2)), statistics1]
                    after[plan["rstd"]] += [rstd1]
                    after[plan["scale"]] += [lambda: scale1(xn_ready)]
                    after[plan["tau"]] += [lambda: tau_of(k + 1)]
                for t in range(T):
                    after[plan["divide"][0][t]].append(lambda t=t: divide(k, 0, t))
                    if post:
                        after[plan["divide"][1][t]].append(lambda t=t: divide(k - 1, 1, t))
                if post:
                    for i in range(2):
                        after[plan["residual"][i]].append(lambda i=i: residual(k - 1, i))
                    after[plan["rstd2"]] += [rstd2]
                    after[plan["scale2"]] += [lambda: scale_rows(k - 1)]
                    after[plan["choose"]] += [lambda: choose(k - 1)]
                    after[plan["notes"]] += [lambda: row_notes(k - 1)]
                    after[plan["places"]] += [lambda: places(k - 1)]
                for u in range(U):
                    shifted_scores(k, u)
                    for step in after[u]:
                        step()

            link = Chain(dve, dve_setup)
            dve.wait_ge(x_loaded, 16)
            statistics1()
            rstd1()
            scale1(xn_ready)
            dve.wait_ge(f_loaded, 16)
            link(dve.tensor_scalar(d_rest[:, 0], d_row, 0.25, None, ALU.mult))
            link(dve.tensor_copy(d_bf3[:, 0:B * KV], d_rest[:, 0]))
            link(dve.tensor_tensor(d_rest[:, 1], d_rest[:, 0], d_bf3[:, 0:B * KV], ALU.subtract))
            link(dve.tensor_copy(d_bf3[:, B * KV:2 * B * KV], d_rest[:, 1]))
            link(dve.tensor_tensor(d_rest[:, 0], d_rest[:, 1], d_bf3[:, B * KV:2 * B * KV], ALU.subtract))
            dve.tensor_copy(d_bf3[:, 2 * B * KV:3 * B * KV], d_rest[:, 0]).then_inc(d_split, 1)
            dve.wait_ge(b_loaded, 96)
            tau_of(0)
            for b in range(B):
                dve.wait_ge(setup_pe, 8 + b)
                dve.tensor_tensor(v[:, b, :], ps[0:KV, 7 if b else 4, 0:D], bv_sb, ALU.add).then_inc(setup_dve, 1)
            dve.wait_ge(consts_ready, 2)
            link = Chain(dve, dve_chain[0])
            body(0, post=False)
            with dve.Fori(1, NBLK - 1) as k:
                link = Chain(dve, dve_chain[1], DVE_CHAIN * (k - 1))
                body(k)
                assert link.n == DVE_CHAIN, link.n
            link = Chain(dve, dve_chain[2])
            body(NBLK - 1, pre=False)

            length, tiles, end, begin, shift, one, taken_early, spare = (tab_s[:, i, :] for i in range(8))

            def over_tiles(row, count):
                return row.rearrange("p (o e) -> p o e", o=1).to_broadcast([1, count, E])

            def tables(early):
                first, count = (0, EARLY) if early else (EARLY, NT - EARLY)
                of_tile = tab_t[:, 0:count]
                if early:
                    dve.wait_ge(pos_ready, NBLK - 1)
                    dve.memset(one, 1.0)
                else:
                    dve.wait_ge(pos_ready, NBLK)
                    dve.tensor_copy(pad_at[:], place[0:1, :]).then_inc(ends_ready, 1)
                link(dve.tensor_tensor(length, place[0:1, :], list_base[:], ALU.subtract))
                if early:
                    link(dve.tensor_scalar(length, length, -float(LIST_TILE - 1), None, ALU.add))
                link(dve.tensor_tensor(tab_jw, length.rearrange("p (e o) -> p e o", o=1).to_broadcast([1, E, MAXT]), tab_j, ALU.is_gt))
                link(dve.tensor_reduce(tiles, tab_jw, AX.X, ALU.add))
                if not early:
                    link(dve.tensor_tensor(tiles, tiles, taken_early, ALU.subtract))
                link(dve.tensor_tensor_scan(end, one, tiles, 0.0, ALU.mult, ALU.add))
                link(dve.tensor_tensor(begin, end, tiles, ALU.subtract))
                link(dve.tensor_scalar(shift, begin, -float(LIST_TILE), -float(DUMMY), ALU.mult, ALU.add))
                link(dve.tensor_tensor(shift, shift, list_base[:], ALU.add))
                if early:
                    dve.tensor_scalar(taken_early, end, float(EARLY), None, ALU.min)
                    link(dve.tensor_scalar(spare, begin, float(EARLY), None, ALU.min))
                    link(dve.tensor_tensor(taken_early, taken_early, spare, ALU.subtract))
                else:
                    link(dve.scalar_tensor_tensor(out=shift, in0=taken_early, scalar=float(LIST_TILE), in1=shift, op0=ALU.mult, op1=ALU.add))
                begun, ended, at = (w[:, 0:count] for w in tab_w)
                expert, row = tab_r[:, 0, 0:count], tab_r[:, 1, 0:count]
                dve.tensor_tensor(begun, over_tiles(begin, count), of_tile, ALU.is_le)
                link(dve.tensor_tensor(ended, over_tiles(end, count), of_tile, ALU.is_le))
                dve.tensor_reduce(expert, ended, AX.X, ALU.add)
                dve.tensor_tensor(begun, begun, ended, ALU.subtract)
                link(dve.scalar_tensor_tensor(out=at, in0=of_tile, scalar=float(LIST_TILE), in1=over_tiles(shift, count), op0=ALU.mult, op1=ALU.add))
                link(dve.tensor_tensor(at, at, begun, ALU.mult))
                link(dve.tensor_reduce(row, at, AX.X, ALU.add))
                dve.tensor_scalar(tile_row[:, first:first + count], row, float(DUMMY), None, ALU.add)
                link(dve.tensor_scalar(tile_w[:, first:first + count], expert, float(E - 1), float(WE), ALU.min, ALU.mult))
                dve.sem_inc(tables_ready, 1)

            def row_rest(t, s):
                dve.wait_ge(lx_high, t + 1)
                dve.tensor_tensor(xT16[:, s, 1, :], ps[:, XB[s], :], xT16[:, s, 0, :], ALU.subtract).then_inc(lx_rest, 1)

            def take_weights(t, s, n):
                dve.wait_ge(list_loaded[s], 16 * n)
                if not isinstance(t, int) or t >= 2:
                    dve.wait_ge(adds_before, t)
                dve.tensor_copy(y_row[:, s, :], x_list[s][:, :, D + 1].bitcast(I32))
                dve.tensor_scalar(y_scale[:, s, :], x_list[s][:, :, D], 1.0 / W_SCALE, None, ALU.mult).then_inc(taken, 1)

            def split_hidden(t, step):
                dve.wait_ge(gelu_ready, NP * t + step + 1)
                dve.tensor_copy(h16[:, step, 0, :], h32[:, step % 2, :]).then_inc(hid_high, 1)
                dve.wait_ge(hid_high, NP * t + step + 1)
                dve.tensor_tensor(h16[:, step, 1, :], h32[:, step % 2, :], h16[:, step, 0, :], ALU.subtract).then_inc(hid_split, 1)

            def results(t, s):
                dve.wait_ge(y_made, t + 1)
                for h in range(SUB):
                    last = dve.tensor_scalar(y[:, s, h, :], ps[:, YB[s], h * D:(h + 1) * D], y_scale[:, s, h:h + 1], None, ALU.mult)
                last.then_inc(y_ready, 1)

            def tile(t, s, rows_at=1, among={}):
                for step in range(NP):
                    split_hidden(t, step)
                    if step == 1:
                        take_weights(t, s, (t + 2) // 2)
                    if step == rows_at:
                        row_rest(t + 1, 1 - s)
                    if step == 1 and not (isinstance(t, int) and t == 0):
                        results(t - 1, 1 - s)
                    if step in among:
                        among[step]()

            def route():
                row_notes(NBLK - 1)
                places(NBLK - 1)

            tables(early=True)
            for t in range(T):
                divide(NBLK - 1, 1, t)
            for i in range(2):
                residual(NBLK - 1, i)
            rstd2()
            scale_rows(NBLK - 1)
            among = {0: {3: lambda: choose(NBLK - 1)}, 1: {0: route, 2: lambda: tables(early=False)}}
            row_rest(0, 0)
            for t in range(EARLY):
                tile(t, t % 2, rows_at(t), among.get(t, {}))
            with dve.Fori(0, (NT - EARLY - 2) // 2) as i:
                for s2 in range(2):
                    tile(2 * i + (s2 + EARLY), (s2 + EARLY) % 2)
            for t in range(EARLY + (NT - EARLY - 2) // 2 * 2, NT):
                tile(t, t % 2, rows_at(t))
            results(NT - 1, (NT - 1) % 2)


_INS = ['x', 'ctx_1024', 'condB_tau', 'fside_BxS2_0', 'L0_xcond_Wq', 'L0_xcond_bq', 'L0_xcond_Wk', 'L0_xcond_bk',
        'L0_xcond_Wv', 'L0_xcond_bv', 'L0_xcond_Wo', 'L0_xcond_bo', 'L0_ffn_gate_w', 'L0_ffn_fc_w', 'L0_ffn_proj_w']


def kernel(**inputs):
    import numpy as _np
    import concourse.bacc as _bacc
    from concourse import mybir as _mybir
    from concourse.bass_utils import run_bass_kernel_spmd as _run

    nc = _bacc.Bacc("TRN2", target_bir_lowering=False, num_devices=1)
    arrays, args = {}, []
    for name in _INS:
        a = _np.ascontiguousarray(inputs[name])
        arrays[f"in_{name}"] = a
        args.append(nc.dram_tensor(f"in_{name}", a.shape, _mybir.dt.from_np(a.dtype), kind="ExternalInput").ap())
    b, s, d = arrays["in_x"].shape
    args.append(nc.dram_tensor("out", (b * s + LIST_PAD, d), F32, kind="ExternalOutput").ap())
    build(nc, *args)
    r = _run(nc, [arrays], core_ids=[0])
    return r.results[0]["out"][:b * s].reshape(b, s, d)
```

```python
from contextlib import ExitStack

import concourse.bass as bass
from concourse import mybir

F32 = mybir.dt.float32
F16 = mybir.dt.float16
BF16 = mybir.dt.bfloat16
I32 = mybir.dt.int32
U32 = mybir.dt.uint32
ALU = mybir.AluOpType
ACT = mybir.ActivationFunctionType
AX = mybir.AxisListType

P = 128
LN_EPS = 1e-5
W_SCALE = 64.0
H = 16
PE_PLAN = {
    "first": dict(first_rows=3, queries=(7, 13), values=((6, 6), (9, 9), (15, 15), (1, 1))),
    "middle": dict(first_rows=3, queries=(7, 13), values=((6, 6), (9, 9), (15, 15), (1, 1)), outputs=(4, 5, 6, 6),
                   second_rows=10, logits=11, ranks=14),
    "last": dict(values=((6, 6), (9, 9), (15, 15), (1, 1)), outputs=(4, 5, 6, 6), second_rows=10, logits=11,
                 ranks=14),
}
ACT_PLAN = {
    "first": dict(first_rows=3, queries=(9, 15)),
    "middle": dict(first_rows=3, queries=(9, 15), second_rows=10, both_rows=15, gap=14),
    "last": dict(second_rows=10, both_rows=15, gap=14),
}
DVE_PLAN = {
    "first": dict(statistics=1, rstd=1, scale=2, tau=4, divide=((10, 12, 13, 14), (2, 3, 3, 5))),
    "middle": dict(statistics=1, rstd=1, scale=2, tau=4, divide=((10, 12, 13, 14), (2, 3, 3, 5)), residual=(7, 8),
                   rstd2=8, scale2=9, choose=14, notes=15, places=15),
    "last": dict(divide=((10, 12, 13, 14), (2, 3, 3, 5)), residual=(7, 8), rstd2=8, scale2=9, choose=14, notes=15,
                 places=15),
}
CHUNKS = {
    "first": (1, 1, 0, 1, 0, 1, 1, 1, 2, 1, 2, 0, 2, 0, 2, 1),
    "middle": (1, 1, 0, 1, 0, 1, 1, 1, 2, 1, 2, 0, 2, 0, 2, 1),
    "last": (1, 1, 0, 1, 0, 1, 1, 1, 2, 1, 2, 0, 2, 0, 2, 1),
}
POOL_PLAN = dict(residual=2, free_rows=4, keys=6)
STORE_AT = 8
LAST_PLAN = dict(second_rows=(0, 1), logits=(0, 3), ranks=(1, 0), tables=(1, 2))
AHEAD = 2
LIST_TILE = 256
LIST_PAD = LIST_TILE


class Chain:

    def __init__(self, eng, sem, base=0):
        self.eng, self.sem, self.base, self.n = eng, sem, base, 0

    def __call__(self, ins):
        self.n += 1
        ins.then_inc(self.sem, 1)
        self.eng.wait_ge(self.sem, self.base + self.n)


def settle(eng, passed):
    eng.sem_inc(passed, 1)


def wait(eng, sem, value):
    if not isinstance(value, int) or value > 0:
        eng.wait_ge(sem, value)


def build(nc, x, ctx_in, tau, fside, Wq, bq, Wk, bk, Wv, bv, Wo, bo, gate_w, fc_w, proj_w, out):
    B, S, D = x.shape
    KV = ctx_in.shape[1]
    E, _, F = fc_w.shape
    DK = D // H
    N = B * S
    T = 4
    BLK = T * P
    NBLK = N // BLK
    HALVES = S // BLK
    KD = D // P
    NG = H // 4
    U = NG * T
    CAP = N + LIST_PAD
    NT = (2 * N + E * (LIST_TILE - 1)) // LIST_TILE
    DUMMY = E * CAP
    EARLY = 4
    assert EARLY * LIST_TILE + E * (LIST_TILE - 1) <= 2 * (N - BLK) + LIST_TILE - 1
    ROW = D + 2
    SUB = LIST_TILE // P
    NP = F // (2 * P)
    WE = 2 * KD * F
    MAXT = N // LIST_TILE
    STAGES = 4
    CH = 512
    assert (KD, DK, SUB, F // P, NBLK) == (2, 16, 2, 8, B * HALVES) and 2 * E * 4 * CH == NBLK * U * CH
    assert E * KD * F * 2 == NBLK * U * CH

    lists = nc.dram_tensor("lists", (E * CAP + LIST_TILE, ROW), F32, kind="Internal").ap()

    with ExitStack() as es:
        def sb(name, shape, dt=F32):
            return es.enter_context(nc.sbuf_tensor(name, shape, dt))

        def sem(name):
            return es.enter_context(nc.semaphore(name))

        ps = es.enter_context(nc.psum_tensor("ps", [P, 8, 512], F32))
        SCORE, PROBT, OUTB, SUMB, SIDE = [0, 1], [4, 5], 6, 7, [2, 3]
        HID, YB, XB = [0, 1], [4, 5], [6, 7]

        ident = sb("ident", [P, P])
        tri = sb("tri", [P, P], BF16)
        ones_bf = sb("ones_bf", [P, P], BF16)
        head_mask = sb("head_mask", [P, 2, 4])
        iota_e = sb("iota_e", [P, E])
        fcw = sb("fcw", [P, E * WE], F16)
        prw = sb("prw", [P, E * WE], F16)
        gate = sb("gate", [P, KD, E])
        wqT = sb("wqT", [P, KD, D])
        woT = sb("woT", [P, KD, D])
        bq_sb = sb("bq_sb", [P, KD])
        bk_sb = sb("bk_sb", [P, KD])
        bo_sb = sb("bo_sb", [P, D])
        tau4 = sb("tau4", [P, B])
        w_stage = sb("w_stage", [P, STAGES, CH])
        kT = sb("kT", [P, KD, B, KV])
        v = sb("v", [KV, B, D])
        kbd = sb("kbd", [P, KD, 2, 4, KV])
        vpad = sb("vpad", [KV, H, 2 * DK])
        ones_pad = sb("ones_pad", [KV, 2, 2 * DK])
        dparts = sb("dparts", [3, B, KV], BF16)
        tau_cur = sb("tau_cur", [P, 1])
        bq_cur = sb("bq_cur", [P, KD])
        x_in = sb("x_in", [P, T, D])
        x1 = sb("x1", [P, T, D])
        xnT = sb("xnT", [P, 2, KD, BLK])
        qT = sb("qT", [P, KD, BLK])
        attnT = sb("attnT", [P, KD, BLK])
        probs = sb("probs", [P, 4, 4, KV])
        nmax = sb("nmax", [P, 2, 4])
        arena = sb("arena", [P, 4096])
        rows = sb("rows", [P, T, 2, ROW])
        stats = sb("stats", [P, T, 6])
        mv = sb("mv", [P, T, 2])
        ln = sb("ln", [P, 5, T])
        top8 = sb("top8", [P, T, 8])
        top8_at = sb("top8_at", [P, T, 8], U32)
        which = sb("which", [P, 2, T])
        chosen = sb("chosen", [P, 2, T, E])
        chosen_bf = sb("chosen_bf", [P, T, E], BF16)
        place_t = sb("place_t", [P, T, E])
        place = sb("place", [P, E])
        list_base = sb("list_base", [1, E])
        pos = sb("pos", [P, 2, T], I32)
        tw = sb("tw", [P, 4, T])
        row_no = sb("row_no", [P, T])
        tile_row = sb("tile_row", [1, NT], I32)
        tile_w = sb("tile_w", [1, NT], I32)
        pad_at = sb("pad_at", [1, E], I32)

        y_row = sb("y_row", [P, 2, SUB], I32)
        y_scale = sb("y_scale", [P, 2, SUB])

        w_nat = arena[:, 0:2048].rearrange("p (w m d) -> p w m d", w=4, m=KD)
        wkvT = arena[:, 2048:3072].rearrange("p (w k d) -> p w k d", w=2, k=KD)
        ctx_nat = arena[0:KV, 3072:3584].rearrange("p (b d) -> p b d", b=B)
        ctxT = arena[:, 3584:3584 + KD * B * KV].rearrange("p (k n) -> p k n", k=KD)
        bv_sb = rows[0:KV, 0, 0, 0:D]
        d_row = rows[0:1, 1, 0, 0:B * KV]
        d_rest = rows[0:1, 2, :, 0:B * KV]
        d_bf3 = rows[0:1, 3, 0, 0:256].bitcast(BF16)[:, 0:3 * B * KV]
        probsT = arena[0:KV, :].rearrange("p (s j n) -> p s j n", s=2, j=4)
        h16 = arena[:, 0:2048].bitcast(F16).rearrange("p (s c n) -> p s c n", s=4, c=2)
        h32 = arena[:, 2048:3072].rearrange("p (s n) -> p s n", s=2)
        xT16 = arena[:, 3072:4096].bitcast(F16).rearrange("p (s c n) -> p s c n", s=2, c=2)
        halves = [qT[:, :, :].rearrange("p k n -> p (k n)"), xnT[:, 0, :, :].rearrange("p k n -> p (k n)")]
        x_list = [h[:, 0:SUB * ROW].rearrange("p (h r) -> p h r", h=SUB) for h in halves]
        tab_q, tab_x = (h[0:1, SUB * ROW:] for h in halves)
        tab_s = tab_q[:, 0:8 * E].rearrange("p (s e) -> p s e", e=E)
        tab_r = tab_q[:, 8 * E:8 * E + 2 * NT].rearrange("p (r t) -> p r t", r=2)
        tab_jw = tab_q[:, 8 * E + 2 * NT:(8 + MAXT) * E + 2 * NT].rearrange("p (e j) -> p e j", e=E)
        tab_w = [tab_x[:, 0:NT * E], tab_x[:, NT * E:2 * NT * E], tab_q[:, 256:256 + NT * E]]
        tab_w = [w.rearrange("p (t e) -> p t e", e=E) for w in tab_w]
        y = x_in[:, :, :].rearrange("p (s h) d -> p s h d", s=2)
        pad_rows = x1[:, :, :].rearrange("p t d -> p (t d)")[:, 0:SUB * ROW].rearrange("p (h r) -> p h r", h=SUB)
        tab_c = kT[0:1, :, :, :].rearrange("p m b k -> p (m b k)")
        tab_t = tab_c[:, 0:NT * E].rearrange("p (t e) -> p t e", e=E)
        tab_j = tab_c[:, NT * E:(NT + MAXT) * E].rearrange("p (e j) -> p e j", e=E)

        ctx_loaded, w_loaded, b_loaded, f_loaded = sem("ctx_loaded"), sem("w_loaded"), sem("b_loaded"), sem("f_loaded")
        x_loaded = sem("x_loaded")
        stage_loaded = [sem(f"stage_loaded{i}") for i in range(STAGES)]
        out_stored = sem("out_stored")
        consts_ready = sem("consts_ready")
        setup_pe, setup_act, setup_dve = sem("setup_pe"), sem("setup_act"), sem("setup_dve")
        d_split, d_moved = sem("d_split"), sem("d_moved")
        keys_ready, values_ready, x_bias_added = sem("keys_ready"), sem("values_ready"), sem("x_bias_added")
        pool_chain, dve_setup = sem("pool_chain"), sem("dve_setup")
        dve_chain = [sem(f"dve_chain{i}") for i in range(3)]
        hid_high, pool_passed, dve_passed, sp_passed = sem("hid_high"), sem("pool_passed"), sem("dve_passed"), sem("sp_passed")
        xn_ready, tau_ready, res_loaded = sem("xn_ready"), sem("tau_ready"), sem("res_loaded")
        xT_made, xT_copied, q_made, q_ready = sem("xT_made"), sem("xT_copied"), sem("q_made"), sem("q_ready")
        scores_made, shifted, probs_ready = sem("scores_made"), sem("shifted"), sem("probs_ready")
        pT_made, pT_copied, pv_made, attn_ready = sem("pT_made"), sem("pT_copied"), sem("pv_made"), sem("attn_ready")
        o_made, x1_ready = sem("o_made"), sem("x1_ready")
        rows_ready, rows_copied, logits_made = sem("rows_ready"), sem("rows_copied"), sem("logits_made")
        gap_ready, exp_ready, chosen_ready, ranks_made = sem("gap_ready"), sem("exp_ready"), sem("chosen_ready"), sem("ranks_made")
        pos_ready, scattered, rows_free = sem("pos_ready"), sem("scattered"), sem("rows_free")
        w_high, w_rest = sem("w_high"), sem("w_rest")
        tables_ready, pads_written = sem("tables_ready"), sem("pads_written")
        pads_made, ends_ready = sem("pads_made"), sem("ends_ready")
        list_loaded = [sem("list_loaded0"), sem("list_loaded1")]
        lx_made, lx_high, lx_rest = sem("lx_made"), sem("lx_high"), sem("lx_rest")
        hid_made, gelu_ready, hid_split, y_made, y_ready = (
            sem("hid_made"), sem("gelu_ready"), sem("hid_split"), sem("y_made"), sem("y_ready"))
        y_added, taken, adds_before = sem("y_added"), sem("taken"), sem("adds_before")

        def kind(post, pre):
            return "middle" if post and pre else "last" if post else "first"

        def chunks_at(kind, u):
            return range(sum(CHUNKS[kind][:u]), sum(CHUNKS[kind][:u + 1]))

        def stage_dram(e, g, t):
            if g % 2 == 0:
                k, half = divmod(t, 2)
                return fc_w[bass.ds(e, 1), k * P:(k + 1) * P, half * CH:(half + 1) * CH].rearrange("e p n -> p (e n)")
            return proj_w[bass.ds(e, 1), 2 * t * P:(2 * t + 2) * P, :].rearrange("e (h p) n -> p (e h) n", p=P)

        def stage_sb(u, g):
            s = w_stage[:, u % STAGES, :]
            return s if g % 2 == 0 else s.rearrange("p (h n) -> p h n", h=2)

        def split_dst(e, g, t, part):
            if g % 2 == 0:
                k, half = divmod(t, 2)
                return fcw[:, bass.ds(e * WE + (2 * k + part) * F + half * CH, CH)]
            w = prw[:, :].rearrange("p (f c n) -> p f c n", c=2, n=D)
            return w[:, bass.ds(e * (F // P) + 2 * t, 2), part, :]

        def rows_at(t):
            return None if t == NT - 1 else NP - 1 if t == EARLY - 1 else 1

        block = es.enter_context(nc.Block())

        @block.sync
        def _(sp):
            x_rows = x.rearrange("b s d -> (b s) d")
            sp.dma_start(x_in[:], x_rows[0:BLK, :].rearrange("(t p) d -> p t d", p=P)).then_inc(x_loaded, 16)
            for i, w in enumerate((Wk, Wv, Wq, Wo)):
                sp.dma_start(w_nat[:, i], w.rearrange("(m p) d -> p m d", p=P)).then_inc(w_loaded, 16)
            sp.dma_start(ctx_nat, ctx_in.rearrange("b k d -> k b d")).then_inc(ctx_loaded, 16)
            sp.dma_start(d_row, fside.rearrange("(a b) k -> a (b k)", a=1)).then_inc(f_loaded, 16)
            sp.dma_start(bk_sb[:], bk.rearrange("(m p) -> p m", p=P), allow_slow_non_contiguous=True).then_inc(b_loaded, 16)
            sp.dma_start(bq_sb[:], bq.rearrange("(m p) -> p m", p=P), allow_slow_non_contiguous=True).then_inc(b_loaded, 16)
            sp.dma_start(bv_sb, bv.rearrange("(a d) -> a d", a=1).to_broadcast([KV, D])).then_inc(b_loaded, 16)
            sp.dma_start(bo_sb[:], bo.rearrange("(a d) -> a d", a=1).to_broadcast([P, D])).then_inc(b_loaded, 16)
            sp.dma_start(tau4[:], tau.rearrange("(a b) -> a b", a=1).to_broadcast([P, B])).then_inc(b_loaded, 16)
            sp.dma_start(gate[:], gate_w.rearrange("(k p) e -> p k e", p=P)).then_inc(b_loaded, 16)
            sp.wait_ge(consts_ready, 1)
            sp.dma_start(out[N:N + LIST_PAD, :].rearrange("(h p) d -> p h d", p=P), pad_rows[:, :, 0:D]).then_inc(out_stored, 16)
            sp.dma_start(lists[DUMMY:DUMMY + LIST_TILE, :].rearrange("(h p) r -> p h r", p=P), pad_rows[:]).then_inc(pads_written, 16)

            def load_block(dst, k, loaded):
                sp.dma_start(dst[:], x_rows[bass.ds(k * BLK, BLK), :].rearrange("(t p) d -> p t d", p=P)).then_inc(loaded, 16)

            def store_x1(k):
                sp.wait_ge(x1_ready, k + 1)
                sp.dma_start(out[bass.ds(k * BLK, BLK), :].rearrange("(t p) d -> p t d", p=P), x1[:]).then_inc(out_stored, 16)

            def body(k, post=True, pre=True):
                def load_next():
                    sp.wait_ge(q_made, KD * k + 1)
                    load_block(x_in, k + 1, x_loaded)

                if pre and post:
                    load_next()
                for c in range(U):
                    g, t = divmod(c, T)
                    wait(sp, w_rest, U * k + c + 1 - STAGES)
                    sp.dma_start(stage_sb(c, g), stage_dram(2 * k + g // 2, g, t)).then_inc(stage_loaded[c % STAGES], 16)
                    if pre and not post and c == STAGES - 1:
                        load_next()
                    if post and c == 0:
                        if not isinstance(k, int):
                            sp.wait_ge(pads_written, 16)
                        sp.wait_ge(q_made, KD * (k + 1))
                        settle(sp, sp_passed)
                        sp.wait_ge(out_stored, 16 * k)
                        load_block(x1, k - 1, res_loaded)
                    if post and c == STORE_AT:
                        store_x1(k - 1)

            body(0, post=False)
            with sp.Fori(1, NBLK - 1) as k:
                body(k)
            body(NBLK - 1, pre=False)
            sp.wait_ge(rows_ready, NBLK - 1)
            sp.wait_ge(out_stored, 16 * NBLK)
            load_block(x1, NBLK - 1, res_loaded)

            def load_tile(t, slot):
                at = sp.value_load(tile_row[0:1, bass.ds(t, 1)], min_val=0, max_val=DUMMY)
                sp.dma_start(x_list[slot], lists[bass.ds(at, LIST_TILE), :].rearrange("(h p) r -> p h r", p=P)).then_inc(list_loaded[slot], 16)

            def load_next_tile(t, slot):
                sp.wait_ge(lx_made, t - 1)
                sp.wait_ge(taken, t - 1)
                load_tile(t, slot)

            sp.wait_ge(tables_ready, 1)
            sp.wait_ge(pv_made, NG * NBLK)
            sp.wait_ge(scattered, 16 * 2 * T * (NBLK - 1))
            for t in range(2):
                load_tile(t, t)
            store_x1(NBLK - 1)
            for t in range(2, EARLY):
                load_next_tile(t, t % 2)
            sp.wait_ge(ends_ready, 1)
            sp.wait_ge(pads_made, 1)
            for e in range(E):
                at = sp.value_load(pad_at[0:1, e:e + 1], min_val=e * CAP, max_val=e * CAP + N)
                sp.dma_start(lists[bass.ds(at, LIST_PAD), :].rearrange("(h p) r -> p h r", p=P), pad_rows[:]).then_inc(pads_written, 16)
            sp.wait_ge(tables_ready, 2)
            sp.wait_ge(pads_written, 16 * (E + 1))
            sp.wait_ge(scattered, 16 * 2 * T * NBLK)
            with sp.Fori(0, (NT - EARLY) // 2) as i:
                for s in range(2):
                    load_next_tile(2 * i + (s + EARLY), (s + EARLY) % 2)
            for t in range(EARLY + (NT - EARLY) // 2 * 2, NT):
                load_next_tile(t, t % 2)
            sp.wait_ge(out_stored, 16 * (NBLK + 1))
            sp.wait_ge(y_added, 16 * SUB * NT)

        @block.gpsimd
        def _(pool):
            link = Chain(pool, pool_chain)

            def make_pads():
                link(pool.memset(pad_rows[:], 0.0))
                link(pool.iota(pad_rows[:, :, D + 1:D + 2].bitcast(I32), pattern=[[P, SUB], [0, 1]], base=N, channel_multiplier=1))

            make_pads()
            link(pool.memset(ident[:], 0.0))
            link(pool.affine_select(out=ident[:], in_=ident[:], compare_op=ALU.not_equal, fill=1.0, base=0,
                                    pattern=[[-1, P]], channel_multiplier=1))
            pool.sem_inc(consts_ready, 1)
            link(pool.memset(ones_bf[:], 1.0))
            link(pool.memset(tri[:], 1.0))
            link(pool.affine_select(out=tri[:], in_=tri[:], compare_op=ALU.is_gt, fill=0.0, base=0,
                                    pattern=[[1, P]], channel_multiplier=-1))
            link(pool.memset(head_mask[:], 1.0))
            link(pool.affine_select(out=head_mask[:], in_=head_mask[:], compare_op=ALU.is_ge, fill=0.0, base=0,
                                    pattern=[[-DK, 2], [-2 * DK, 4]], channel_multiplier=1))
            link(pool.affine_select(out=head_mask[:], in_=head_mask[:], compare_op=ALU.is_ge, fill=0.0, base=DK - 1,
                                    pattern=[[DK, 2], [2 * DK, 4]], channel_multiplier=-1))
            for dst, base_step in ((iota_e, 1), (place, CAP), (list_base, CAP)):
                link(pool.iota(dst[:], pattern=[[base_step, E]], base=0, channel_multiplier=0, allow_small_or_imprecise_dtypes=True))
            link(pool.iota(row_no[:], pattern=[[P, T]], base=0, channel_multiplier=1, allow_small_or_imprecise_dtypes=True))
            link(pool.memset(ones_pad[:], 0.0))
            link(pool.memset(vpad[:], 0.0))
            for par in range(2):
                link(pool.memset(ones_pad[:, par, par * DK:(par + 1) * DK], 1.0))
            pool.sem_inc(consts_ready, 1)
            def batch_keys(b, m):
                wait(pool, scores_made, U * HALVES * b - (0 if m or not b else U // 2))
                pool.tensor_tensor(kbd[:, m].rearrange("p a j k -> p (a j) k"),
                                   kT[:, m, b:b + 1, :].to_broadcast([P, 8, KV]),
                                   head_mask[:].rearrange("p a (j o) -> p (a j) o", o=1).to_broadcast([P, 8, KV]), ALU.mult).then_inc(keys_ready, 1)

            def batch_values(b):
                wait(pool, pv_made, NG * HALVES * b)
                for par in range(2):
                    last = pool.tensor_copy(vpad[:, par::2, par * DK:(par + 1) * DK],
                                            v[:, b, :].rearrange("p (h d) -> p h d", h=H)[:, par::2, :])
                last.then_inc(values_ready, 1)

            def weight_rest(k, c):
                g, t = divmod(c, T)
                pool.wait_ge(w_high, U * k + c + 1)
                pool.tensor_tensor(split_dst(2 * k + g // 2, g, t, 1), stage_sb(c, g), split_dst(2 * k + g // 2, g, t, 0), ALU.subtract).then_inc(w_rest, 1)

            def residual_bias(k):
                pool.wait_ge(res_loaded, 16 * (k + 1))
                pool.tensor_tensor(x1[:], x1[:], bo_sb[:].rearrange("p (o d) -> p o d", o=1).to_broadcast([P, T, D]), ALU.add).then_inc(x_bias_added, 1)

            def scatter(k):
                pool.wait_ge(rows_copied, k + 1)
                pool.wait_ge(pos_ready, k + 1)
                settle(pool, pool_passed)
                for s in range(2):
                    for t in range(T):
                        pool.indirect_dma_start(lists[:, :], bass.IndirectOffsetOnAxis(ap=pos[:, s, t:t + 1], axis=0),
                                                rows[:, t, s, :], None).then_inc(scattered, 16)

            def free_rows(k):
                pool.wait_ge(scattered, 16 * 2 * T * (k + 1))
                pool.sem_inc(rows_free, 1)

            for m in range(KD):
                pool.wait_ge(setup_act, 6 + m)
                batch_keys(0, m)
            pool.wait_ge(d_moved, 48)
            pool.wait_ge(setup_dve, B)
            pool.sem_inc(rows_free, 1)
            batch_values(0)
            for k in range(NBLK):
                if k >= 2:
                    scatter(k - 2)
                if k and k % HALVES == 0:
                    batch_keys(k // HALVES, 1)
                    batch_values(k // HALVES)
                    if k // HALVES == B - 1:
                        pool.wait_ge(keys_ready, KD * B)
                        link(pool.iota(tab_j[:], pattern=[[0, E], [LIST_TILE, MAXT]], base=0, channel_multiplier=0, allow_small_or_imprecise_dtypes=True))
                        link(pool.iota(tab_t[:], pattern=[[1, NT], [0, E]], base=0, channel_multiplier=0, allow_small_or_imprecise_dtypes=True))
                for c in range(U):
                    if c == U - 2 and k == NBLK - 1:
                        residual_bias(k)
                        scatter(k - 1)
                    weight_rest(k, c)
                    if c == POOL_PLAN["residual"] and k >= 1:
                        residual_bias(k - 1)
                    if c == POOL_PLAN["free_rows"] and k >= 2:
                        free_rows(k - 2)
                    if c == POOL_PLAN["keys"] and (k + 1) % HALVES == 0 and k + 1 < NBLK:
                        batch_keys((k + 1) // HALVES, 0)
            free_rows(NBLK - 2)
            pool.wait_ge(rows_ready, NBLK)
            pool.wait_ge(out_stored, 16 * (NBLK + 1))
            make_pads()
            pool.sem_inc(pads_made, 1)
            scatter(NBLK - 1)

            def add_tile(t, s, first=False):
                if not first:
                    pool.wait_ge(y_added, 16 * SUB * t)
                pool.sem_inc(adds_before, 1)
                pool.wait_ge(y_ready, t + 1)
                settle(pool, pool_passed)
                for h in range(SUB):
                    pool.indirect_dma_start(out[:, :], bass.IndirectOffsetOnAxis(ap=y_row[:, s, h:h + 1], axis=0),
                                            y[:, s, h, :], None, compute_op=ALU.add).then_inc(y_added, 16)

            add_tile(0, 0, first=True)
            with pool.Fori(0, (NT - 1) // 2) as i:
                for s2 in range(2):
                    add_tile(2 * i + s2 + 1, (s2 + 1) % 2)
            pool.wait_ge(y_added, 16 * SUB * NT)

        @block.tensor
        def _(pe):
            pe.wait_ge(consts_ready, 1)
            pe.wait_ge(w_loaded, 64)
            for w in range(4):
                for k in range(KD):
                    for m in range(KD):
                        last = pe.transpose(ps[:, w, k * D + m * P:k * D + (m + 1) * P], w_nat[:, w, m, k * P:(k + 1) * P], ident[:])
                last.then_inc(setup_pe, 1)
            pe.wait_ge(ctx_loaded, 16)
            for k in range(KD):
                for b in range(B):
                    last = pe.transpose(ps[:, 4, (k * B + b) * KV:(k * B + b + 1) * KV], ctx_nat[:, b, k * P:(k + 1) * P], ident[0:KV, 0:KV])
            last.then_inc(setup_pe, 1)

            def transposed(src, n):
                for c in range(KD):
                    for t in range(T):
                        last = pe.transpose(ps[:, SIDE[c], t * P:(t + 1) * P], src[:, t, c * P:(c + 1) * P], ident[:])
                    last.then_inc(xT_made, 1)

            def first_rows(k, n):
                pe.wait_ge(xn_ready, k + 1)
                transposed(x_in, n)

            pe.wait_ge(setup_act, 4)
            first_rows(0, 1)
            pe.wait_ge(setup_act, 5)
            for m in range(KD):
                for k in range(KD):
                    last = pe.matmul(ps[:, 5 + m, 0:B * KV], wkvT[:, 0, k, m * P:(m + 1) * P], ctxT[:, k, :], start=(k == 0), stop=(k == KD - 1))
                last.then_inc(setup_pe, 1)
            for b in range(B):
                for k in range(KD):
                    last = pe.matmul(ps[0:KV, 7 if b else 4, 0:D], ctxT[:, k, b * KV:(b + 1) * KV], wkvT[:, 1, k, :], start=(k == 0), stop=(k == KD - 1))
                last.then_inc(setup_pe, 1)
            pe.wait_ge(consts_ready, 2)

            def project_queries(m, n):
                pe.wait_ge(xT_copied, KD * n)
                for c in range(KD):
                    last = pe.matmul(ps[:, SIDE[m], :], wqT[:, c, m * P:(m + 1) * P], xnT[:, 0, c, :], start=(c == 0), stop=(c == KD - 1))
                last.then_inc(q_made, 1)

            def scores(k, u):
                g, t = divmod(u, T)
                m, par = divmod(g, 2)
                if u % (U // 2) == 0:
                    pe.wait_ge(q_ready, KD * k + m + 1)
                    pe.wait_ge(keys_ready, KD * (k // HALVES) + m + 1)
                wait(pe, shifted, U * k + u - 1)
                o = ps[:, SCORE[u % 2], 0:4 * KV]
                pe.matmul(o, qT[:, m, t * P:(t + 1) * P], kbd[:, m, par].rearrange("p j k -> p (j k)"), start=True, stop=False)
                pe.matmul(o, ones_bf[0:3, :], dparts[:, bass.ds(k // HALVES, 1), :].to_broadcast([3, 4, KV]), start=False, stop=True).then_inc(scores_made, 1)

            def transpose_probs(k, u):
                pe.wait_ge(probs_ready, U * k + u + 1)
                wait(pe, pT_copied, U * k + u - 1)
                for j in range(4):
                    last = pe.transpose(ps[0:KV, PROBT[u % 2], j * P:(j + 1) * P], probs[:, u % 4, j, :], ident[:])
                last.then_inc(pT_made, 1)

            def weigh_values(k, g, parts=(0, 1)):
                m, par = divmod(g, 2)
                if 0 in parts:
                    pe.wait_ge(pT_copied, U * k + T * (g + 1))
                    if g == 0:
                        pe.wait_ge(values_ready, k // HALVES + 1)
                    if par == 0:
                        wait(pe, attn_ready, T * (KD * k + m))
                for part in parts:
                    for j in range(4):
                        last = pe.matmul(ps[2 * DK * j:2 * DK * (j + 1), (OUTB, SUMB)[part], :],
                                         ones_pad[:, par, :] if part else vpad[:, 8 * m + 2 * j + par, :],
                                         probsT[:, g % 2, j, :], start=(par == 0), stop=(par == 1))
                if 1 in parts:
                    last.then_inc(pv_made, 1)

            def project_outputs(k, t):
                pe.wait_ge(attn_ready, T * (KD * k + 1) + t + 1)
                for m in range(KD):
                    last = pe.matmul(ps[:, SIDE[t // 2], (t % 2) * D:(t % 2 + 1) * D], attnT[:, m, t * P:(t + 1) * P], woT[:, m, :],
                                     start=(m == 0), stop=(m == KD - 1))
                if t % 2:
                    last.then_inc(o_made, 1)

            def second_rows(k, n):
                pe.wait_ge(rows_ready, k + 1)
                transposed(rows[:, :, 0, :], n)

            def logits(n):
                pe.wait_ge(xT_copied, KD * n)
                for t in range(T):
                    for c in range(KD):
                        last = pe.matmul(ps[:, SIDE[0], t * E:(t + 1) * E], xnT[:, 1, c, t * P:(t + 1) * P], gate[:, c, :], start=(c == 0), stop=(c == KD - 1))
                last.then_inc(logits_made, 1)

            def ranks(k):
                pe.wait_ge(chosen_ready, k + 1)
                pe.matmul(ps[:, SIDE[0], 0:T * E], tri[:], chosen_bf[:].rearrange("p t e -> p (t e)"), start=True, stop=False, skip_group_check=True)
                for t in range(T - 1):
                    later = T - 1 - t
                    pe.matmul(ps[:, SIDE[0], (t + 1) * E:T * E].rearrange("p (t e) -> p t e", e=E), ones_bf[:],
                              chosen_bf[:, t:t + 1, :].to_broadcast([P, later, E]), start=False, stop=(t == T - 2), skip_group_check=True)
                for t in range(T):
                    last = pe.matmul(ps[:, SIDE[0], T * E:(T + 1) * E], ones_bf[:], chosen_bf[:, t, :], start=(t == 0), stop=(t == T - 1),
                                     skip_group_check=True)
                last.then_inc(ranks_made, 1)

            def body(k, post=True, pre=True):
                plan = PE_PLAN[kind(post, pre)]
                n_first, n_second = (2 * k + 1 if post else 2), (2 * k + 2 if pre else 2 * k + 1)
                if not post:
                    pe.wait_ge(d_moved, 48)
                    pe.wait_ge(setup_dve, B)
                    scores(k, 0)
                    scores(k, 1)
                for u in range(U):
                    if u + 2 < U:
                        scores(k, u + 2)
                    elif pre:
                        scores(k + 1, u + 2 - U)
                    if u >= 1:
                        transpose_probs(k, u - 1)
                    elif post:
                        transpose_probs(k - 1, U - 1)
                    if post:
                        weigh_values(k - 1, NG - 1, [part for part in range(2) if u == plan["values"][3][part]])
                    if not post and u == 0:
                        project_queries(1, 1)
                    if not post and u == plan["first_rows"]:
                        pe.wait_ge(q_ready, KD)
                    if pre and u == plan["first_rows"]:
                        first_rows(k + 1, n_first)
                    if post and u == plan["outputs"][0]:
                        if pre:
                            pe.wait_ge(xT_copied, KD * n_first)
                        else:
                            pe.wait_ge(pos_ready, k - 1)
                    for t in range(T):
                        if post and u == plan["outputs"][t]:
                            project_outputs(k - 1, t)
                    weigh_values(k, 0, [part for part in range(2) if u == plan["values"][0][part]])
                    if pre and u == plan["queries"][0]:
                        if post:
                            pe.wait_ge(x1_ready, k)
                        project_queries(0, n_first)
                    weigh_values(k, 1, [part for part in range(2) if u == plan["values"][1][part]])
                    if post and u == plan["second_rows"]:
                        if pre:
                            pe.wait_ge(q_ready, KD * (k + 1) + 1)
                        second_rows(k - 1, n_second)
                    if post and u == plan["logits"]:
                        logits(n_second)
                    if post and u == plan["ranks"]:
                        ranks(k - 1)
                    if pre and u == plan["queries"][1]:
                        project_queries(1, n_first)
                    weigh_values(k, 2, [part for part in range(2) if u == plan["values"][2][part]])

            project_queries(0, 1)
            body(0, post=False)
            with pe.Fori(1, NBLK - 1) as k:
                body(k)
            body(NBLK - 1, pre=False)
            transpose_probs(NBLK - 1, U - 1)
            weigh_values(NBLK - 1, NG - 1)
            pe.wait_ge(pos_ready, NBLK - 1)
            for t in range(T):
                project_outputs(NBLK - 1, t)

            pe.wait_ge(tables_ready, 1)
            pe.wait_ge(w_high, NBLK * U)
            pe.wait_ge(w_rest, NBLK * U)

            def list_rows(t, s, n):
                pe.wait_ge(list_loaded[s], 16 * n)
                for k in range(KD):
                    for h in range(SUB):
                        last = pe.transpose(ps[:, XB[s], (k * SUB + h) * P:(k * SUB + h + 1) * P], x_list[s][:, h, k * P:(k + 1) * P], ident[:])
                last.then_inc(lx_made, 1)

            def hidden(t, s, step, w):
                if step == 0:
                    pe.wait_ge(lx_rest, t + 1)
                wait(pe, gelu_ready, NP * t + step - 1)
                for f2 in range(2):
                    f = 2 * step + f2
                    o = ps[:, HID[step % 2], f2 * LIST_TILE:(f2 + 1) * LIST_TILE]
                    n = 0
                    for k in range(KD):
                        for wp, xp in ((0, 0), (0, 1), (1, 0)):
                            last = pe.matmul(o, fcw[:, bass.ds(w + ((2 * k + wp) * F + f * P), P)],
                                             xT16[:, s, xp, k * LIST_TILE:(k + 1) * LIST_TILE], start=(n == 0), stop=(n == 3 * KD - 1))
                            n += 1
                last.then_inc(hid_made, 1)

            def outputs(t, s, step, w):
                pe.wait_ge(hid_split, NP * t + step + 1)
                for f2 in range(2):
                    for wp, hp in ((0, 0), (0, 1), (1, 0)):
                        for h in range(SUB):
                            first = (step, f2, wp, hp, h) == (0, 0, 0, 0, 0)
                            final = (step, f2, wp) == (NP - 1, 1, 1)
                            last = pe.matmul(ps[:, YB[s], h * D:(h + 1) * D],
                                             h16[:, step, hp, f2 * LIST_TILE + h * P:f2 * LIST_TILE + (h + 1) * P],
                                             prw[:, bass.ds(w + (2 * (2 * step + f2) + wp) * D, D)],
                                             start=first, stop=final, skip_group_check=True)
                if step == NP - 1:
                    last.then_inc(y_made, 1)

            def weights_of(t):
                return pe.value_load(tile_w[0:1, bass.ds(t, 1)], min_val=0, max_val=(E - 1) * WE)

            LAG = 2

            def last_steps(at):
                if at == LAST_PLAN["second_rows"]:
                    second_rows(NBLK - 1, 2 * NBLK)
                if at == LAST_PLAN["logits"]:
                    logits(2 * NBLK)
                if at == LAST_PLAN["ranks"]:
                    ranks(NBLK - 1)

            def tile(t, s, w_last, rows_at=1, early=False):
                w = weights_of(t)
                for step in range(NP):
                    hidden(t, s, step, w)
                    if step == rows_at:
                        list_rows(t + 1, 1 - s, (t + 3) // 2)
                    if step >= LAG:
                        outputs(t, s, step - LAG, w)
                    elif w_last is not None:
                        outputs(t - 1, 1 - s, NP - LAG + step, w_last)
                    if early:
                        last_steps((t, step))

            list_rows(0, 0, 1)
            for t in range(EARLY):
                tile(t, t % 2, weights_of(t - 1) if t else None, rows_at(t), early=True)
            pe.wait_ge(tables_ready, 2)
            with pe.Fori(0, (NT - EARLY - 2) // 2) as i:
                for s2 in range(2):
                    t = 2 * i + (s2 + EARLY)
                    tile(t, (s2 + EARLY) % 2, weights_of(t - 1))
            for t in range(EARLY + (NT - EARLY - 2) // 2 * 2, NT):
                tile(t, t % 2, weights_of(t - 1), rows_at(t))
            w = weights_of(NT - 1)
            for step in range(NP - LAG, NP):
                outputs(NT - 1, (NT - 1) % 2, step, w)

        @block.scalar
        def _(act):
            for i, dst in enumerate((wkvT[:, 0], wkvT[:, 1], wqT[:], woT[:])):
                act.wait_ge(setup_pe, i + 1)
                act.copy(dst, ps[:, i, :].rearrange("p (k d) -> p k d", k=KD)).then_inc(setup_act, 1)
            act.wait_ge(setup_pe, 5)
            act.copy(ctxT, ps[:, 4, 0:KD * B * KV].rearrange("p (k n) -> p k n", k=KD)).then_inc(setup_act, 1)
            def copy_rows(n, second):
                for c in range(KD):
                    act.wait_ge(xT_made, KD * (n - 1) + c + 1)
                    act.copy(xnT[:, second, c, :], ps[:, SIDE[c], :]).then_inc(xT_copied, 1)

            copy_rows(1, 0)
            act.wait_ge(b_loaded, 96)
            for m in range(KD):
                act.wait_ge(setup_pe, 6 + m)
                act.activation(kT[:, m].rearrange("p b k -> p (b k)"), ps[:, 5 + m, 0:B * KV], ACT.Identity, bias=bk_sb[:, m:m + 1]).then_inc(setup_act, 1)
            for i in range(3):
                act.wait_ge(d_split, 1)
                act.dma_start(dparts[i:i + 1, :, :].rearrange("p b k -> p (b k)"), d_bf3[:, i * B * KV:(i + 1) * B * KV]).then_inc(d_moved, 16)

            def copy_queries(k, m):
                if m == 0:
                    act.wait_ge(tau_ready, k + 1)
                act.wait_ge(q_made, KD * k + m + 1)
                act.activation(qT[:, m, :], ps[:, SIDE[m], :], ACT.Identity, bias=bq_cur[:, m:m + 1], scale=tau_cur[:, 0:1]).then_inc(q_ready, 1)

            def exponentials(k, u):
                act.wait_ge(shifted, U * k + u + 1)
                act.activation(probs[:, u % 4], probs[:, u % 4], ACT.Exp).then_inc(probs_ready, 1)

            def copy_probs(k, u):
                act.wait_ge(pT_made, U * k + u + 1)
                g, t = divmod(u, T)
                if t == 0:
                    wait(act, pv_made, NG * k + g - 1)
                act.copy(probsT[:, g % 2, :, t * P:(t + 1) * P], ps[0:KV, PROBT[u % 2], :].rearrange("p (j n) -> p j n", j=4)).then_inc(pT_copied, 1)

            def weight_high(k, c):
                g, t = divmod(c, T)
                act.wait_ge(stage_loaded[c % STAGES], 16 * (U // STAGES * k + c // STAGES + 1))
                act.activation(split_dst(2 * k + g // 2, g, t, 0), stage_sb(c, g), ACT.Copy, scale=W_SCALE)
                act.activation(w_stage[:, c % STAGES, :], w_stage[:, c % STAGES, :], ACT.Copy, scale=W_SCALE).then_inc(w_high, 1)

            def both_rows(k):
                act.wait_ge(rows_ready, k + 1)
                act.copy(rows[:, :, 1, 0:D], rows[:, :, 0, 0:D]).then_inc(rows_copied, 1)

            def gap_exponential(k):
                act.wait_ge(gap_ready, k + 1)
                act.activation(tw[:, 1, :], tw[:, 0, :], ACT.Exp).then_inc(exp_ready, 1)

            def body(k, post=True, pre=True):
                plan = ACT_PLAN[kind(post, pre)]
                n_first, n_second = (2 * k + 1 if post else 2), (2 * k + 2 if pre else 2 * k + 1)
                for u in range(U):
                    exponentials(k, u)
                    if u >= 2:
                        copy_probs(k, u - 2)
                    elif post:
                        copy_probs(k - 1, U + u - 2)
                    if not post and u == 0:
                        copy_queries(0, 1)
                    for c in chunks_at(kind(post, pre), u):
                        if post or c >= AHEAD:
                            weight_high(k, c)
                    if pre and u == plan["first_rows"]:
                        copy_rows(n_first, 0)
                    if pre and u == plan["queries"][0]:
                        copy_queries(k + 1, 0)
                    if post and u == plan["second_rows"]:
                        copy_rows(n_second, 1)
                    if post and u == plan["both_rows"]:
                        both_rows(k - 1)
                    if post and u == plan["gap"]:
                        gap_exponential(k - 1)
                    if pre and u == plan["queries"][1]:
                        copy_queries(k + 1, 1)

            for c in range(AHEAD):
                weight_high(0, c)
            copy_queries(0, 0)
            body(0, post=False)
            with act.Fori(1, NBLK - 1) as k:
                body(k)
            body(NBLK - 1, pre=False)
            for u in (U - 2, U - 1):
                copy_probs(NBLK - 1, u)
            def row_high(t, s):
                act.wait_ge(lx_made, t + 1)
                act.copy(xT16[:, s, 0, :], ps[:, XB[s], :]).then_inc(lx_high, 1)

            def gelu(t, step):
                act.wait_ge(hid_made, NP * t + step + 1)
                wait(act, hid_split, NP * t + step - 1)
                act.activation(h32[:, step % 2, :], ps[:, HID[step % 2], :], ACT.Gelu, scale=1.0 / W_SCALE).then_inc(gelu_ready, 1)

            def last_steps(at):
                if at == LAST_PLAN["second_rows"]:
                    copy_rows(2 * NBLK, 1)
                    both_rows(NBLK - 1)
                if at == LAST_PLAN["logits"]:
                    gap_exponential(NBLK - 1)

            def tile(t, s, rows_at=1, early=False):
                for step in range(NP):
                    gelu(t, step)
                    if step == rows_at:
                        row_high(t + 1, 1 - s)
                    if early:
                        last_steps((t, step))

            row_high(0, 0)
            for t in range(EARLY):
                tile(t, t % 2, rows_at(t), early=True)
            with act.Fori(0, (NT - EARLY - 2) // 2) as i:
                for s2 in range(2):
                    tile(2 * i + (s2 + EARLY), (s2 + EARLY) % 2)
            for t in range(EARLY + (NT - EARLY - 2) // 2 * 2, NT):
                tile(t, t % 2, rows_at(t))

        @block.vector
        def _(dve):
            DVE_CHAIN = 66

            def rows_norm(src, dst):
                def statistics(ts=range(T)):
                    for t in ts:
                        last = dve.bn_stats(stats[:, t, :], src[:, t, :])
                    link(last)
                    if T - 1 in ts:
                        settle(dve, dve_passed)
                        for t in range(T):
                            last = dve.bn_aggr(mv[:, t, :], stats[:, t, :])
                        link(last)

                def rstd():
                    var, half_bits, r, a, b = (ln[:, i, :] for i in range(5))
                    link(dve.tensor_scalar(var, mv[:, :, 1], LN_EPS, None, ALU.add))
                    link(dve.tensor_scalar(half_bits.bitcast(I32), var.bitcast(I32), 1, None, ALU.logical_shift_right))
                    link(dve.tensor_scalar(r.bitcast(I32), half_bits.bitcast(I32), -1.0, float(0x5F3759DF), ALU.mult, ALU.add))
                    for _ in range(3):
                        link(dve.scalar_tensor_tensor(out=a, in0=var, scalar=-0.5, in1=r, op0=ALU.mult, op1=ALU.mult))
                        link(dve.tensor_tensor(b, a, r, ALU.mult))
                        link(dve.scalar_tensor_tensor(out=r, in0=b, scalar=1.5, in1=r, op0=ALU.add, op1=ALU.mult))

                def scale(ready):
                    for t in range(T):
                        last = dve.tensor_scalar(dst(t), src[:, t, :], mv[:, t, 0:1], ln[:, 2, t:t + 1], ALU.subtract, ALU.mult)
                    last.then_inc(ready, 1)

                return statistics, rstd, scale

            statistics1, rstd1, scale1 = rows_norm(x_in, lambda t: x_in[:, t, :])
            statistics2, rstd2, scale2 = rows_norm(x1, lambda t: rows[:, t, 0, 0:D])

            def tau_of(k):
                wait(dve, q_ready, KD * k)
                link(dve.tensor_scalar(tau_cur[:], tau4[:, bass.ds(k // HALVES, 1)], 0.25, None, ALU.mult))
                dve.tensor_scalar(bq_cur[:], bq_sb[:], tau_cur[:, 0:1], None, ALU.mult).then_inc(tau_ready, 1)

            def shifted_scores(k, u):
                s = ps[:, SCORE[u % 2], 0:4 * KV].rearrange("p (j k) -> p j k", j=4)
                dve.wait_ge(scores_made, U * k + u + 1)
                link(dve.tensor_reduce(nmax[:, u % 2, :], s, AX.X, ALU.max, negate=True))
                wait(dve, pT_made, U * k + u - 3)
                dve.tensor_tensor(probs[:, u % 4], s, nmax[:, u % 2, :].rearrange("p (j o) -> p j o", o=1).to_broadcast([P, 4, KV]), ALU.add).then_inc(shifted, 1)

            def divide(k, m, t):
                dve.wait_ge(pv_made, NG * k + 2 * m + 2)
                n = slice(t * P, (t + 1) * P)
                link(dve.reciprocal(attnT[:, m, n], ps[:, SUMB, n]))
                dve.tensor_tensor(attnT[:, m, n], ps[:, OUTB, n], attnT[:, m, n], ALU.mult).then_inc(attn_ready, 1)

            def residual(k, i):
                if i == 0:
                    dve.wait_ge(x_bias_added, k + 1)
                dve.wait_ge(o_made, 2 * k + i + 1)
                ts = range(2 * i, 2 * i + 2)
                link(dve.tensor_tensor(x1[:, 2 * i:2 * i + 2, :], ps[:, SIDE[i], :].rearrange("p (t d) -> p t d", t=2), x1[:, 2 * i:2 * i + 2, :], ALU.add))
                if i == 1:
                    dve.sem_inc(x1_ready, 1)
                    settle(dve, dve_passed)
                statistics2(ts)

            def choose(k):
                dve.wait_ge(logits_made, k + 1)
                settle(dve, dve_passed)
                lg = ps[:, SIDE[0], 0:T * E].rearrange("p (t e) -> p t e", t=T)
                for t in range(T):
                    last = dve.max(top8[:, t, :], lg[:, t, :])
                link(last)
                settle(dve, dve_passed)
                for t in range(T):
                    last = dve.max_index(top8_at[:, t, :], top8[:, t, :], lg[:, t, :])
                link(last)
                dve.tensor_tensor(tw[:, 0, :], top8[:, :, 1], top8[:, :, 0], ALU.subtract).then_inc(gap_ready, 1)
                link(dve.tensor_copy(which[:].rearrange("p s t -> p t s"), top8_at[:, :, 0:2]))
                for s in range(2):
                    last = dve.tensor_tensor(chosen[:, s], which[:, s, :].rearrange("p (t o) -> p t o", o=1).to_broadcast([P, T, E]),
                                             iota_e[:].rearrange("p (o e) -> p o e", o=1).to_broadcast([P, T, E]), ALU.is_equal)
                link(last)
                dve.tensor_tensor(chosen_bf[:], chosen[:, 0], chosen[:, 1], ALU.add).then_inc(chosen_ready, 1)

            def row_notes(k):
                dve.wait_ge(exp_ready, k + 1)
                link(dve.tensor_scalar(tw[:, 2, :], tw[:, 1, :], 1.0, None, ALU.add))
                link(dve.reciprocal(tw[:, 3, :], tw[:, 2, :]))
                dve.tensor_copy(rows[:, :, 0, D], tw[:, 3, :])
                dve.tensor_tensor(rows[:, :, 1, D], tw[:, 1, :], tw[:, 3, :], ALU.mult)
                for s in range(2):
                    last = dve.tensor_copy(rows[:, :, s, D + 1].bitcast(I32), row_no[:])
                link(last)
                dve.tensor_scalar(row_no[:], row_no[:], float(BLK), None, ALU.add)

            def places(k):
                dve.wait_ge(ranks_made, k + 1)
                link(dve.tensor_tensor(place_t[:], ps[:, SIDE[0], 0:T * E].rearrange("p (t e) -> p t e", t=T),
                                       place[:].rearrange("p (o e) -> p o e", o=1).to_broadcast([P, T, E]), ALU.add))
                dve.tensor_tensor(place[:], ps[:, SIDE[0], T * E:(T + 1) * E], place[:], ALU.add)
                for s in range(2):
                    last = dve.tensor_tensor(chosen[:, s], chosen[:, s], place_t[:], ALU.mult)
                link(last)
                for s in range(2):
                    last = dve.tensor_reduce(which[:, s, :], chosen[:, s], AX.X, ALU.add)
                link(last)
                dve.tensor_copy(pos[:], which[:]).then_inc(pos_ready, 1)

            def scale_rows(k):
                dve.wait_ge(rows_free, k + 1)
                scale2(rows_ready)

            def body(k, post=True, pre=True):
                plan = DVE_PLAN[kind(post, pre)]
                for u in range(U):
                    shifted_scores(k, u)
                    if pre:
                        if u == plan["statistics"]:
                            dve.wait_ge(x_loaded, 16 * (k + 2))
                            statistics1()
                        if u == plan["rstd"]:
                            rstd1()
                        if u == plan["scale"]:
                            scale1(xn_ready)
                        if u == plan["tau"]:
                            tau_of(k + 1)
                    for t in range(T):
                        if u == plan["divide"][0][t]:
                            divide(k, 0, t)
                        if post and u == plan["divide"][1][t]:
                            divide(k - 1, 1, t)
                    if post:
                        for i in range(2):
                            if u == plan["residual"][i]:
                                residual(k - 1, i)
                        if u == plan["rstd2"]:
                            rstd2()
                        if u == plan["scale2"]:
                            scale_rows(k - 1)
                        if u == plan["choose"]:
                            choose(k - 1)
                        if u == plan["notes"]:
                            row_notes(k - 1)
                        if u == plan["places"]:
                            places(k - 1)

            link = Chain(dve, dve_setup)
            dve.wait_ge(x_loaded, 16)
            statistics1()
            rstd1()
            scale1(xn_ready)
            dve.wait_ge(f_loaded, 16)
            link(dve.tensor_scalar(d_rest[:, 0], d_row, 0.25, None, ALU.mult))
            link(dve.tensor_copy(d_bf3[:, 0:B * KV], d_rest[:, 0]))
            link(dve.tensor_tensor(d_rest[:, 1], d_rest[:, 0], d_bf3[:, 0:B * KV], ALU.subtract))
            link(dve.tensor_copy(d_bf3[:, B * KV:2 * B * KV], d_rest[:, 1]))
            link(dve.tensor_tensor(d_rest[:, 0], d_rest[:, 1], d_bf3[:, B * KV:2 * B * KV], ALU.subtract))
            dve.tensor_copy(d_bf3[:, 2 * B * KV:3 * B * KV], d_rest[:, 0]).then_inc(d_split, 1)
            dve.wait_ge(b_loaded, 96)
            tau_of(0)
            for b in range(B):
                dve.wait_ge(setup_pe, 8 + b)
                dve.tensor_tensor(v[:, b, :], ps[0:KV, 7 if b else 4, 0:D], bv_sb, ALU.add).then_inc(setup_dve, 1)
            dve.wait_ge(consts_ready, 2)
            link = Chain(dve, dve_chain[0])
            body(0, post=False)
            with dve.Fori(1, NBLK - 1) as k:
                link = Chain(dve, dve_chain[1], DVE_CHAIN * (k - 1))
                body(k)
                assert link.n == DVE_CHAIN, link.n
            link = Chain(dve, dve_chain[2])
            body(NBLK - 1, pre=False)

            length, tiles, end, begin, shift, one, taken_early, spare = (tab_s[:, i, :] for i in range(8))

            def over_tiles(row, count):
                return row.rearrange("p (o e) -> p o e", o=1).to_broadcast([1, count, E])

            def tables(early):
                first, count = (0, EARLY) if early else (EARLY, NT - EARLY)
                of_tile = tab_t[:, 0:count]
                if early:
                    dve.wait_ge(pos_ready, NBLK - 1)
                    dve.memset(one, 1.0)
                else:
                    dve.wait_ge(pos_ready, NBLK)
                    dve.tensor_copy(pad_at[:], place[0:1, :]).then_inc(ends_ready, 1)
                link(dve.tensor_tensor(length, place[0:1, :], list_base[:], ALU.subtract))
                if early:
                    link(dve.tensor_scalar(length, length, -float(LIST_TILE - 1), None, ALU.add))
                link(dve.tensor_tensor(tab_jw, length.rearrange("p (e o) -> p e o", o=1).to_broadcast([1, E, MAXT]), tab_j, ALU.is_gt))
                link(dve.tensor_reduce(tiles, tab_jw, AX.X, ALU.add))
                if not early:
                    link(dve.tensor_tensor(tiles, tiles, taken_early, ALU.subtract))
                link(dve.tensor_tensor_scan(end, one, tiles, 0.0, ALU.mult, ALU.add))
                link(dve.tensor_tensor(begin, end, tiles, ALU.subtract))
                link(dve.tensor_scalar(shift, begin, -float(LIST_TILE), -float(DUMMY), ALU.mult, ALU.add))
                link(dve.tensor_tensor(shift, shift, list_base[:], ALU.add))
                if early:
                    dve.tensor_scalar(taken_early, end, float(EARLY), None, ALU.min)
                    link(dve.tensor_scalar(spare, begin, float(EARLY), None, ALU.min))
                    link(dve.tensor_tensor(taken_early, taken_early, spare, ALU.subtract))
                else:
                    link(dve.scalar_tensor_tensor(out=shift, in0=taken_early, scalar=float(LIST_TILE), in1=shift, op0=ALU.mult, op1=ALU.add))
                begun, ended, at = (w[:, 0:count] for w in tab_w)
                expert, row = tab_r[:, 0, 0:count], tab_r[:, 1, 0:count]
                dve.tensor_tensor(begun, over_tiles(begin, count), of_tile, ALU.is_le)
                link(dve.tensor_tensor(ended, over_tiles(end, count), of_tile, ALU.is_le))
                dve.tensor_reduce(expert, ended, AX.X, ALU.add)
                dve.tensor_tensor(begun, begun, ended, ALU.subtract)
                link(dve.scalar_tensor_tensor(out=at, in0=of_tile, scalar=float(LIST_TILE), in1=over_tiles(shift, count), op0=ALU.mult, op1=ALU.add))
                link(dve.tensor_tensor(at, at, begun, ALU.mult))
                link(dve.tensor_reduce(row, at, AX.X, ALU.add))
                dve.tensor_scalar(tile_row[:, first:first + count], row, float(DUMMY), None, ALU.add)
                link(dve.tensor_scalar(tile_w[:, first:first + count], expert, float(E - 1), float(WE), ALU.min, ALU.mult))
                dve.sem_inc(tables_ready, 1)

            def take_weights(t, s, n):
                dve.wait_ge(list_loaded[s], 16 * n)
                if not isinstance(t, int) or t >= 2:
                    dve.wait_ge(adds_before, t)
                dve.tensor_copy(y_row[:, s, :], x_list[s][:, :, D + 1].bitcast(I32))
                dve.tensor_scalar(y_scale[:, s, :], x_list[s][:, :, D], 1.0 / W_SCALE, None, ALU.mult).then_inc(taken, 1)

            def split_hidden(t, step):
                dve.wait_ge(gelu_ready, NP * t + step + 1)
                dve.tensor_copy(h16[:, step, 0, :], h32[:, step % 2, :]).then_inc(hid_high, 1)
                dve.wait_ge(hid_high, NP * t + step + 1)
                dve.tensor_tensor(h16[:, step, 1, :], h32[:, step % 2, :], h16[:, step, 0, :], ALU.subtract).then_inc(hid_split, 1)

            def results(t, s):
                dve.wait_ge(y_made, t + 1)
                for h in range(SUB):
                    last = dve.tensor_scalar(y[:, s, h, :], ps[:, YB[s], h * D:(h + 1) * D], y_scale[:, s, h:h + 1], None, ALU.mult)
                last.then_inc(y_ready, 1)

            def last_steps(at):
                if at == LAST_PLAN["logits"]:
                    choose(NBLK - 1)
                if at == LAST_PLAN["ranks"]:
                    row_notes(NBLK - 1)
                    places(NBLK - 1)
                if at == LAST_PLAN["tables"]:
                    tables(early=False)

            def tile(t, s, rows_at=1, early=False):
                for step in range(NP):
                    split_hidden(t, step)
                    if step == 1:
                        take_weights(t, s, (t + 2) // 2)
                    if step == rows_at:
                        row_rest(t + 1, 1 - s)
                    if step == 1 and not (isinstance(t, int) and t == 0):
                        results(t - 1, 1 - s)
                    if early:
                        last_steps((t, step))

            def row_rest(t, s):
                dve.wait_ge(lx_high, t + 1)
                dve.tensor_tensor(xT16[:, s, 1, :], ps[:, XB[s], :], xT16[:, s, 0, :], ALU.subtract).then_inc(lx_rest, 1)

            tables(early=True)
            for t in range(T):
                divide(NBLK - 1, 1, t)
            for i in range(2):
                residual(NBLK - 1, i)
            rstd2()
            row_rest(0, 0)
            scale_rows(NBLK - 1)
            for t in range(EARLY):
                tile(t, t % 2, rows_at(t), early=True)
            with dve.Fori(0, (NT - EARLY - 2) // 2) as i:
                for s2 in range(2):
                    tile(2 * i + (s2 + EARLY), (s2 + EARLY) % 2)
            for t in range(EARLY + (NT - EARLY - 2) // 2 * 2, NT):
                tile(t, t % 2, rows_at(t))
            results(NT - 1, (NT - 1) % 2)


_INS = ['x', 'ctx_1024', 'condB_tau', 'fside_BxS2_0', 'L0_xcond_Wq', 'L0_xcond_bq', 'L0_xcond_Wk', 'L0_xcond_bk',
        'L0_xcond_Wv', 'L0_xcond_bv', 'L0_xcond_Wo', 'L0_xcond_bo', 'L0_ffn_gate_w', 'L0_ffn_fc_w', 'L0_ffn_proj_w']


def kernel(**inputs):
    import numpy as _np
    import concourse.bacc as _bacc
    from concourse import mybir as _mybir
    from concourse.bass_utils import run_bass_kernel_spmd as _run

    nc = _bacc.Bacc("TRN2", target_bir_lowering=False, num_devices=1)
    arrays, args = {}, []
    for name in _INS:
        a = _np.ascontiguousarray(inputs[name])
        arrays[f"in_{name}"] = a
        args.append(nc.dram_tensor(f"in_{name}", a.shape, _mybir.dt.from_np(a.dtype), kind="ExternalInput").ap())
    b, s, d = arrays["in_x"].shape
    args.append(nc.dram_tensor("out", (b * s + LIST_PAD, d), F32, kind="ExternalOutput").ap())
    build(nc, *args)
    r = _run(nc, [arrays], core_ids=[0])
    return r.results[0]["out"][:b * s].reshape(b, s, d)
```
